# Optimizing a Trainium2 kernel written in Bass

```python
import numpy as np
import jax
import jax.numpy as jnp

def _softmax(x, axis=-1):
    return jax.nn.softmax(x, axis=axis)

def _gelu(x):
    return jax.nn.gelu(x, approximate=True)

def _silu(x):
    return jax.nn.silu(x)

def _sigmoid(x):
    return jax.nn.sigmoid(x)

def _layernorm(x, axis=-1, eps=1e-05):
    m = jnp.mean(x, axis=axis, keepdims=True)
    v = jnp.var(x, axis=axis, keepdims=True)
    return (x - m) / jnp.sqrt(v + eps)

def _scatter_add(tgt, idx, src, axis=0):
    return tgt.at[idx].add(src)

def _segment_sum(src, seg, n):
    return jax.ops.segment_sum(src, seg, n)
kernel_name = 'mk_xattn_ffn_d1_seqx_r8_f188b9'

def setup_inputs(seed: int=0):
    np.random.seed(seed)
    _w = jnp.asarray

    def _rec_inputs():
        import jax
        import jax.numpy as jnp
        _rk = jax.random.key(seed)
        x = 0.000341 + 1 * jax.random.normal(jax.random.fold_in(_rk, 1), (8, 128, 256), jnp.float32)
        _lenS = 128 - jax.random.randint(jax.random.fold_in(_rk, 7), (8,), 0, max(1, 128 // 4) + 1, jnp.int32)
        _lenS2 = 128 - jax.random.randint(jax.random.fold_in(_rk, 8), (8,), 0, max(1, 128 // 4) + 1, jnp.int32)
        _ctx_2048P = jax.random.normal(jax.random.fold_in(_rk, 11), (8, 16, 256), jnp.float32)
        _ctx_2048c = jax.random.dirichlet(jax.random.fold_in(_rk, 511), 0.3 * jnp.ones((16,), jnp.float32), (8, 128))
        _ctx_2048t = jnp.einsum('bsk,bkd->bsd', _ctx_2048c, _ctx_2048P)
        _ctx_2048t = _ctx_2048t * jax.lax.rsqrt(jnp.mean(jnp.square(_ctx_2048t)) + 1e-12) * 0.953939
        ctx_2048 = -1.47943e-05 + 1.00017 * (_ctx_2048t + 0.3 * jax.random.normal(jax.random.fold_in(_rk, 611), (8, 128, 256), jnp.float32))
        return (x, ctx_2048)
    x, ctx_2048 = _rec_inputs()

    def _L0_xattn_setup():
        import jax, jax.numpy as jnp
        import numpy as np

        def _wkv(time_decay, time_first, k, v):
            w = -jnp.exp(time_decay)
            u = time_first
            B, T, C = k.shape
            aa = jnp.zeros((B, C), dtype=k.dtype)
            bb = jnp.zeros((B, C), dtype=k.dtype)
            pp = jnp.full((B, C), -1e+38, dtype=k.dtype)

            def step(carry, kv_t):
                aa, bb, pp = carry
                kt, vt = kv_t
                ww = u + kt
                q = jnp.maximum(pp, ww)
                e1 = jnp.exp(pp - q)
                e2 = jnp.exp(ww - q)
                y_t = (e1 * aa + e2 * vt) / (e1 * bb + e2)
                ww2 = pp + w
                q2 = jnp.maximum(ww2, kt)
                e1b = jnp.exp(ww2 - q2)
                e2b = jnp.exp(kt - q2)
                new_carry = (e1b * aa + e2b * vt, e1b * bb + e2b, q2)
                return (new_carry, y_t)
            ks = jnp.transpose(k, (1, 0, 2))
            vs = jnp.transpose(v, (1, 0, 2))
            _, ys = jax.lax.scan(step, (aa, bb, pp), (ks, vs))
            return jnp.transpose(ys, (1, 0, 2))
        key = jax.random.key(seed)
        k1, k2, k3, k4 = jax.random.split(key, 4)
        B, T, C = (8, 128, 256)
        return {'batch_size': B, 'seq_len': T, 'embedding_dim': C, 'time_decay': jax.random.normal(k1, (C,), dtype=jnp.float32), 'time_first': jax.random.normal(k2, (C,), dtype=jnp.float32), 'k': jax.random.normal(k3, (B, T, C), dtype=jnp.float32), 'v': jax.random.normal(k4, (B, T, C), dtype=jnp.float32)}
    _L0_xattn_all = _L0_xattn_setup()
    _L0_xattn_in = {k: v for k, v in _L0_xattn_all.items() if k in ('time_decay', 'time_first')}
    del _L0_xattn_all

    def _L0_ffn_setup():
        import jax, jax.numpy as jnp
        import numpy as np
        H = 256
        I = 128
        E = 32
        K = 4
        N_SHARED = 1
        EPS = 1e-06

        def _rmsnorm(x, w, eps=EPS):
            var = jnp.mean(jnp.square(x), axis=-1, keepdims=True)
            return x * jax.lax.rsqrt(var + eps) * w

        def _moe_core(x, gate_w, w13, w2):
            T = x.shape[0]
            N = T * K
            C = 2 * N // E
            logits = jnp.einsum('th,eh->te', x.astype(jnp.float32), gate_w.astype(jnp.float32))
            scores = jax.nn.softmax(logits, axis=-1)
            topk_w, topk_ids = jax.lax.top_k(scores, K)
            topk_w = topk_w / jnp.sum(topk_w, axis=-1, keepdims=True)
            flat_ids = topk_ids.reshape(-1)
            flat_w = topk_w.reshape(-1)
            order = jnp.argsort(flat_ids)
            sorted_eid = flat_ids[order]
            tok = order // K
            counts = jnp.zeros((E,), jnp.int32).at[flat_ids].add(1)
            starts = jnp.cumsum(counts) - counts
            pos = jnp.arange(N) - starts[sorted_eid]
            buf = jnp.zeros((E, C, x.shape[1]), x.dtype).at[sorted_eid, pos].set(x[tok], mode='drop')
            gu = jnp.einsum('ech,ehf->ecf', buf, w13)
            g, u = jnp.split(gu, 2, axis=-1)
            act = jax.nn.silu(g) * u
            eo = jnp.einsum('eci,eih->ech', act, w2)
            out_slots = eo[sorted_eid, pos]
            routed = jnp.zeros_like(x).at[tok].add(out_slots * flat_w[order][:, None])
            return routed
        key = jax.random.key(seed)
        ks = jax.random.split(key, 8)
        s = 1.0 / np.sqrt(H)
        si = 1.0 / np.sqrt(I)
        return {'hidden_states': jax.random.normal(ks[0], (1, 512, H), jnp.float32), 'norm_w': jnp.ones((H,), jnp.float32), 'gate_w': jax.random.normal(ks[1], (E, H), jnp.float32) * s, 'w13': jax.random.normal(ks[2], (E, H, 2 * I), jnp.float32) * s, 'w2': jax.random.normal(ks[3], (E, I, H), jnp.float32) * si, 'shared_gate_w': jax.random.normal(ks[4], (H, I * N_SHARED), jnp.float32) * s, 'shared_up_w': jax.random.normal(ks[5], (H, I * N_SHARED), jnp.float32) * s, 'shared_down_w': jax.random.normal(ks[6], (I * N_SHARED, H), jnp.float32) * si}
    _L0_ffn_all = _L0_ffn_setup()
    _L0_ffn_in = {k: v for k, v in _L0_ffn_all.items() if k in ('norm_w', 'gate_w', 'w13', 'w2', 'shared_gate_w', 'shared_up_w', 'shared_down_w')}
    del _L0_ffn_all
    return {'x': x, 'ctx_2048': ctx_2048, 'L0_xattn_time_decay': _L0_xattn_in['time_decay'], 'L0_xattn_time_first': _L0_xattn_in['time_first'], 'L0_ffn_norm_w': _L0_ffn_in['norm_w'], 'L0_ffn_gate_w': _L0_ffn_in['gate_w'], 'L0_ffn_w13': _L0_ffn_in['w13'], 'L0_ffn_w2': _L0_ffn_in['w2'], 'L0_ffn_shared_gate_w': _L0_ffn_in['shared_gate_w'], 'L0_ffn_shared_up_w': _L0_ffn_in['shared_up_w'], 'L0_ffn_shared_down_w': _L0_ffn_in['shared_down_w']}

def reference(x, ctx_2048, L0_xattn_time_decay, L0_xattn_time_first, L0_ffn_norm_w, L0_ffn_gate_w, L0_ffn_w13, L0_ffn_w2, L0_ffn_shared_gate_w, L0_ffn_shared_up_w, L0_ffn_shared_down_w):
    import jax
    import jax.numpy as jnp

    def _L0_xattn_ref(batch_size, seq_len, embedding_dim, time_decay, time_first, k, v):
        import jax, jax.numpy as jnp
        import numpy as np

        def _wkv(time_decay, time_first, k, v):
            w = -jnp.exp(time_decay)
            u = time_first
            B, T, C = k.shape
            aa = jnp.zeros((B, C), dtype=k.dtype)
            bb = jnp.zeros((B, C), dtype=k.dtype)
            pp = jnp.full((B, C), -1e+38, dtype=k.dtype)

            def step(carry, kv_t):
                aa, bb, pp = carry
                kt, vt = kv_t
                ww = u + kt
                q = jnp.maximum(pp, ww)
                e1 = jnp.exp(pp - q)
                e2 = jnp.exp(ww - q)
                y_t = (e1 * aa + e2 * vt) / (e1 * bb + e2)
                ww2 = pp + w
                q2 = jnp.maximum(ww2, kt)
                e1b = jnp.exp(ww2 - q2)
                e2b = jnp.exp(kt - q2)
                new_carry = (e1b * aa + e2b * vt, e1b * bb + e2b, q2)
                return (new_carry, y_t)
            ks = jnp.transpose(k, (1, 0, 2))
            vs = jnp.transpose(v, (1, 0, 2))
            _, ys = jax.lax.scan(step, (aa, bb, pp), (ks, vs))
            return jnp.transpose(ys, (1, 0, 2))
        assert seq_len <= 128
        return _wkv(time_decay, time_first, k, v)

    def _L0_ffn_ref(hidden_states, norm_w, gate_w, w13, w2, shared_gate_w, shared_up_w, shared_down_w):
        import jax, jax.numpy as jnp
        import numpy as np
        H = 256
        I = 128
        E = 32
        K = 4
        N_SHARED = 1
        EPS = 1e-06

        def _rmsnorm(x, w, eps=EPS):
            var = jnp.mean(jnp.square(x), axis=-1, keepdims=True)
            return x * jax.lax.rsqrt(var + eps) * w

        def _moe_core(x, gate_w, w13, w2):
            T = x.shape[0]
            N = T * K
            C = 2 * N // E
            logits = jnp.einsum('th,eh->te', x.astype(jnp.float32), gate_w.astype(jnp.float32))
            scores = jax.nn.softmax(logits, axis=-1)
            topk_w, topk_ids = jax.lax.top_k(scores, K)
            topk_w = topk_w / jnp.sum(topk_w, axis=-1, keepdims=True)
            flat_ids = topk_ids.reshape(-1)
            flat_w = topk_w.reshape(-1)
            order = jnp.argsort(flat_ids)
            sorted_eid = flat_ids[order]
            tok = order // K
            counts = jnp.zeros((E,), jnp.int32).at[flat_ids].add(1)
            starts = jnp.cumsum(counts) - counts
            pos = jnp.arange(N) - starts[sorted_eid]
            buf = jnp.zeros((E, C, x.shape[1]), x.dtype).at[sorted_eid, pos].set(x[tok], mode='drop')
            gu = jnp.einsum('ech,ehf->ecf', buf, w13)
            g, u = jnp.split(gu, 2, axis=-1)
            act = jax.nn.silu(g) * u
            eo = jnp.einsum('eci,eih->ech', act, w2)
            out_slots = eo[sorted_eid, pos]
            routed = jnp.zeros_like(x).at[tok].add(out_slots * flat_w[order][:, None])
            return routed
        B, S, Hd = hidden_states.shape
        residual = hidden_states
        h = _rmsnorm(hidden_states, norm_w)
        x = h.reshape(-1, Hd)
        routed = _moe_core(x, gate_w, w13, w2)
        shared = jax.nn.silu(x @ shared_gate_w) * (x @ shared_up_w) @ shared_down_w
        out = residual + (routed + shared).reshape(B, S, Hd)
        return out
    x = x + _L0_xattn_ref(8, 128, 256, L0_xattn_time_decay, L0_xattn_time_first, _layernorm(x, axis=-1), ctx_2048)
    x = x + _L0_ffn_ref(_layernorm(x, axis=-1), L0_ffn_norm_w, L0_ffn_gate_w, L0_ffn_w13, L0_ffn_w2, L0_ffn_shared_gate_w, L0_ffn_shared_up_w, L0_ffn_shared_down_w)
    return x

_drawn_inputs = setup_inputs


def setup_inputs(seed=0):
    import zlib

    import numpy as np

    out = dict(_drawn_inputs(seed))
    spreads = {'L0_ffn_norm_w': (1.0, 0.2)}
    factors = {}
    for name, (base, spread) in spreads.items():
        noise = np.random.default_rng([zlib.crc32(name.encode()), seed]).standard_normal(out[name].shape)
        drawn = base * np.exp(spread * noise) if base else spread * noise
        out[name] = jnp.asarray(drawn.astype(out[name].dtype))
    for name, factor in factors.items():
        out[name] = (out[name] * factor).astype(out[name].dtype)
    return out
```

```python
import concourse.bass as bass
from concourse import mybir
from contextlib import ExitStack

F32 = mybir.dt.float32
BF16 = mybir.dt.bfloat16
I32 = mybir.dt.int32
U32 = mybir.dt.uint32
ALU = mybir.AluOpType
ACT = mybir.ActivationFunctionType
AX = mybir.AxisListType

P = 128
B, T, C = 8, 128, 256
E, K, F = 32, 4, 128
CAP = 2 * B * T * K // E
HC = C // P
SLOTS = E * CAP
LN_EPS, RMS_EPS = 1e-5, 1e-6
OVER = 4 * SLOTS
U_MAX = 60.0
NR = 4
WB = 4


def xattn_moe(nc, x, ctx_in, time_decay, time_first, norm_w, gate_w, w13, w2, sh_gate, sh_up, sh_down, out):
    ctx = ExitStack()
    with ctx:
        def sb(name, shape, dt=F32):
            return ctx.enter_context(nc.sbuf_tensor(name, shape, dt))

        def sem(name):
            return ctx.enter_context(nc.semaphore(name))

        rows_in = nc.dram_tensor("rows_in", (SLOTS, C), F32, kind="Internal").ap()
        rows_out = nc.dram_tensor("rows_out", (SLOTS, C), F32, kind="Internal").ap()

        x_all = sb("x_all", [P, B, C])
        v_all = sb("v_all", [P, B, C])
        base_all = sb("base_all", [P, B, C])
        hT_all = sb("hT_all", [P, HC, B, T])
        w_all = sb("w_all", [P, B, K])
        gslot_all = sb("gslot_all", [P, B * K], I32)

        ident = sb("ident", [P, P])
        tri = sb("tri", [P, P], BF16)
        ones = sb("ones", [P, P], BF16)
        iota_e = sb("iota_e", [P, E])
        slot0 = sb("slot0", [P, E])
        rows6 = sb("rows6", [3 * HC, P])
        cols6 = sb("cols6", [P, 3 * HC])
        td, tf, nw = (cols6[:, HC * m:HC * (m + 1)] for m in range(3))
        etd = sb("etd", [P, HC])
        dcol = sb("dcol", [P, HC])
        ucol = sb("ucol", [P, HC])
        tfc = sb("tfc", [P, HC])
        decay = sb("decay", [P, 2, HC, T])
        gw = sb("gw", [E, C])
        gwT = sb("gwT", [P, HC, E])
        sgu = sb("sgu", [P, HC, 2, F])
        sdn = sb("sdn", [P, C])
        zeros = sb("zeros", [P, 1024])
        neg_half = sb("neg_half", [P, B])

        st1 = sb("st1", [P, B, 6])
        mv1 = sb("mv1", [P, B, 2])
        ve1 = sb("ve1", [P, B])
        rstd1 = sb("rstd1", [P, B])
        nb1 = sb("nb1", [P, B])

        ek = sb("ek", [P, 2, C])
        ekv = sb("ekv", [P, 2, C])
        S = sb("S", [P, 2, 2, HC, T])
        ND = sb("ND", [P, 2, 2, HC, T])
        R = sb("R", [P, 2, HC, T])
        Y = sb("Y", [P, 2, HC, T])
        x1 = sb("x1", [P, 2, C])
        st2 = sb("st2", [P, 2, 6])
        mv2 = sb("mv2", [P, 2, 2])
        ve2 = sb("ve2", [P, 2, 2])
        rs2 = sb("rs2", [P, 2, 3])
        mr2 = sb("mr2", [P, 2, 2])
        nb2 = sb("nb2", [P, 2, 2])
        n_row = sb("n_row", [P, NR, C])
        hT = sb("hT", [P, 2, HC, T])
        top8 = sb("top8", [P, 2, 8])
        idx8 = sb("idx8", [P, 2, 8], U32)
        idxf = sb("idxf", [P, 2, K])
        nmax = sb("nmax", [P, 2, 1])
        ew = sb("ew", [P, 2, K])
        esum = sb("esum", [P, 2, 1])
        rsum = sb("rsum", [P, 2, 1])
        onehot = sb("onehot", [P, 2, K, E])
        mask = sb("mask", [P, 2, E], BF16)
        before = sb("before", [P, 2, E], BF16)
        slots = sb("slots", [P, 2, 2, E])
        over = sb("over", [P, 2, E])
        picked = sb("picked", [P, 2, 2, K, E])
        slotf = sb("slotf", [P, 2, 2, K])
        gslot = sb("gslot", [P, 2, K], I32)
        sslot = sb("sslot", [P, NR, K], I32)

        w13b = [sb(f"w13b{q}", [P, HC, 2, F]) for q in range(WB)]
        w2b = [sb(f"w2b{q}", [P, C]) for q in range(WB)]
        xg = [sb(f"xg{q}", [P, 2, C]) for q in range(WB)]
        xT = sb("xT", [P, 2, HC, CAP])
        sg = sb("sg", [P, 2, CAP])
        act_t = sb("act_t", [P, 2, CAP])
        yo = sb("yo", [P, WB, 2, C])
        G = sb("G", [P, 2, K, C])
        res = sb("res", [P, 2, C])
        part = sb("part", [P, 2, K, C])

        bank = [ctx.enter_context(nc.psum_tensor(f"bank{i}", [P, 512], F32)) for i in range(8)]
        XT = [bank[j][:, :].rearrange("p (a h t) -> p a h t", a=2, h=HC) for j in range(2)]
        YT = [bank[2 + j][:, 0:C] for j in range(2)]
        NT = [bank[4 + j][:, 0:C].rearrange("p (h t) -> p h t", h=HC) for j in range(2)]
        LG = bank[6][:, 0:E]
        PO = bank[7][:, 0:E]
        GWT = bank[6][:, 256:256 + HC * E].rearrange("p (h e) -> p h e", h=HC)
        COLT = bank[7][:, 256:256 + 3 * HC]
        FX = [bank[j][:, :].rearrange("p (h s) -> p h s", h=HC) for j in range(2)]
        FG = [bank[2 + j][:, :].rearrange("p (a s) -> p a s", a=2) for j in range(2)]
        FY = [bank[4 + j][:, :].rearrange("p (a c) -> p a c", a=2) for j in range(2)]

        names = """held_pool colT_ready cols6_done x0_in x1_in v0_in v1_in col_in gw_in sh_in zero_set zeroed consts ident_set tri_set
            st1_done mv1_done ve1_done rstd1_done nb1_done decay_e tf_clamped cols_done decay_done gwT_ready gwT_done
            ek_ready ekv_ready xt_ready col0_done scan_done nd_done recip_done y_ready yt_ready x1_ready st2_done
            mv2_done ve2_done rs2_done mr2_done nb2_done n_ready base_ready nt_ready hT_ready hTall_done lg_ready
            top_ready idx_done idxf_done nmax_done ew_ready rsum_done w_done onehot_done mask_ready before_ready
            pos_ready ga_done over_done slots_done picked_done slotf_done sslot_ready gslot_ready gslot_set
            sh_g sh_s sh_a sh_y sh_b f_xt f_x f_g f_s f_a f_y f_yo tail_part out_free res_ready""".split()
        s = {n: sem(n) for n in names}
        scattered = [sem(f"scattered{r}") for r in range(NR)]
        w_in = [sem(f"w_in{q}") for q in range(WB)]
        xg_in = [sem(f"xg_in{q}") for q in range(WB)]
        stored = [sem(f"stored{q}") for q in range(WB)]
        gathered = [sem(f"gathered{j}") for j in range(2)]
        out_done = [sem(f"out_done{j}") for j in range(2)]

        def run(stages):
            for n in range(min(lag for lag, _ in stages), B + max(lag for lag, _ in stages)):
                for lag, stage in stages:
                    if 0 <= n - lag < B:
                        stage(n - lag, (n - lag) % 2)

        block = ctx.enter_context(nc.Block())

        @block.sync
        def _(sp):
            xv = x.rearrange("b t c -> t b c")
            vv = ctx_in.rearrange("b t c -> t b c")
            h = B // 2
            sp.dma_start(x_all[:, 0:h, :], xv[:, 0:h, :]).then_inc(s["x0_in"], 16)
            sp.dma_start(x_all[:, h:B, :], xv[:, h:B, :]).then_inc(s["x1_in"], 16)
            sp.dma_start(v_all[:, 0:h, :], vv[:, 0:h, :]).then_inc(s["v0_in"], 16)
            sp.dma_start(v_all[:, h:B, :], vv[:, h:B, :]).then_inc(s["v1_in"], 16)
            sp.dma_start(gw[:, :], gate_w).then_inc(s["gw_in"], 16)
            sp.dma_start(sgu[:, :, 0, :], sh_gate.rearrange("(h p) f -> p h f", p=P)).then_inc(s["sh_in"], 16)
            sp.dma_start(sgu[:, :, 1, :], sh_up.rearrange("(h p) f -> p h f", p=P)).then_inc(s["sh_in"], 16)
            sp.dma_start(sdn[:, :], sh_down).then_inc(s["sh_in"], 16)
            sp.wait_ge(s["zero_set"], 1)
            zv = rows_in.rearrange("(a p r) c -> a p (r c)", p=P, r=4)
            for a in range(SLOTS // (4 * P)):
                sp.dma_start(zv[a], zeros[:, :]).then_inc(s["zeroed"], 16)

            def load_weights(e, q):
                sp.dma_start(w13b[q][:, :, :, :].rearrange("p h a f -> p h (a f)"),
                             w13[bass.ds(e, 1)].rearrange("o (h p) f -> p (o h) f", p=P)).then_inc(w_in[q], 16)
                sp.dma_start(w2b[q][:, :], w2[bass.ds(e, 1)].rearrange("o p c -> p (o c)")).then_inc(w_in[q], 16)

            def load_rows(e, q):
                sp.dma_start(xg[q][:, :, :],
                             rows_in[bass.ds(e * CAP, CAP), :].rearrange("(a p) c -> p a c", p=P)).then_inc(xg_in[q], 16)

            def store_rows(e, q, n):
                sp.wait_ge(s["f_yo"], e + 1)
                sp.dma_start(rows_out[bass.ds(e * CAP, CAP), :].rearrange("(a p) c -> p a c", p=P),
                             yo[:, q, :, :]).then_inc(stored[q], 16)

            for q in range(WB):
                load_weights(q, q)
            for r in range(NR):
                sp.wait_ge(scattered[r], 16 * K * B // NR)
            for q in range(WB):
                load_rows(q, q)
            with sp.Fori(0, E // WB - 1) as i:
                for q in range(WB):
                    e = WB * i + q
                    store_rows(e, q, i)
                    load_weights(e + WB, q)
                    load_rows(e + WB, q)
            for q in range(WB):
                store_rows(E - WB + q, q, E // WB - 1)
            ov = out.rearrange("b t c -> t b c")
            with sp.Fori(0, B // 2) as i:
                for j in range(2):
                    b = 2 * i + j
                    sp.wait_ge(s["res_ready"], b + 1)
                    sp.dma_start(ov[:, bass.ds(b, 1), :], res[:, j:j + 1, :]).then_inc(out_done[j], 16)
            for j in range(2):
                sp.wait_ge(out_done[j], 16 * B // 2)

        @block.gpsimd
        def _(pool):
            pool.memset(zeros[:, :], 0.0).then_inc(s["zero_set"], 1)
            pool.memset(ident[:, :], 0.0).then_inc(s["ident_set"], 1)
            pool.memset(tri[:, :], 1.0).then_inc(s["tri_set"], 1)
            pool.memset(ones[:, :], 1.0).then_inc(s["consts"], 1)
            pool.memset(neg_half[:, :], -0.5).then_inc(s["consts"], 1)
            pool.memset(before[:, 0, :], 0.0).then_inc(s["before_ready"], 1)
            pool.iota(iota_e[:, :], [[1, E]], base=0, channel_multiplier=0,
                      allow_small_or_imprecise_dtypes=True).then_inc(s["consts"], 1)
            pool.iota(slot0[:, :], [[CAP, E]], base=0, channel_multiplier=0,
                      allow_small_or_imprecise_dtypes=True).then_inc(s["consts"], 1)
            pool.wait_ge(s["ident_set"], 1)
            pool.affine_select(out=ident[:, :], in_=ident[:, :], compare_op=ALU.not_equal, fill=1.0, base=0,
                               pattern=[[-1, P]], channel_multiplier=1).then_inc(s["ident_set"], 1)
            pool.wait_ge(s["tri_set"], 1)
            pool.affine_select(out=tri[:, :], in_=tri[:, :], compare_op=ALU.is_gt, fill=0.0, base=0,
                               pattern=[[1, P]], channel_multiplier=-1).then_inc(s["tri_set"], 1)
            pool.wait_ge(s["mv1_done"], B)
            pool.tensor_scalar(ve1[:, :], mv1[:, :, 1], LN_EPS, 1.0, ALU.add, ALU.mult).then_inc(s["ve1_done"], 1)
            pool.wait_ge(s["ve1_done"], 1)
            pool.wait_ge(s["consts"], 4)
            pool.tensor_tensor(rstd1[:, :], ve1[:, :], neg_half[:, :], ALU.pow).then_inc(s["rstd1_done"], 1)
            pool.wait_ge(s["v0_in"], 16)
            pool.wait_ge(s["v1_in"], 16)

            def times_v(b, j):
                pool.wait_ge(s["ek_ready"], b + 1)
                pool.tensor_tensor(ekv[:, j, :], ek[:, j, :], v_all[:, bass.ds(b, 1), :].rearrange("p o c -> p (o c)"),
                                   ALU.mult).then_inc(s["ekv_ready"], 1)

            def norm_scales(b, j):
                pool.wait_ge(s["mv2_done"], b + 1)
                pool.tensor_scalar(ve2[:, j, 0:1], mv2[:, j, 1:2], 1.0, LN_EPS, ALU.mult, ALU.add).then_inc(s["ve2_done"], 1)
                pool.tensor_scalar(ve2[:, j, 1:2], mv2[:, j, 1:2], 1.0 + RMS_EPS, LN_EPS * RMS_EPS,
                                   ALU.mult, ALU.add).then_inc(s["ve2_done"], 1)
                pool.wait_ge(s["ve2_done"], 2 * b + 2)
                pool.tensor_tensor(rs2[:, j, 0:2], ve2[:, j, :], neg_half[:, 0:2], ALU.pow).then_inc(s["rs2_done"], 1)
                pool.wait_ge(s["rs2_done"], 2 * b + 1)
                pool.tensor_scalar(rs2[:, j, 2:3], rs2[:, j, 0:1], 1.0, 1.0, ALU.mult, ALU.add).then_inc(s["rs2_done"], 1)
                pool.tensor_scalar(nb2[:, j, :], rs2[:, j, 0:2], mv2[:, j, 0:1], -1.0, ALU.mult, ALU.mult)\
                    .then_inc(s["nb2_done"], 1)

            def count(b, j):
                pool.wait_ge(s["mask_ready"], b + 1)
                pool.wait_ge(s["before_ready"], b + 1)
                pool.wait_ge(s["pos_ready"], b + 1)
                pool.tensor_tensor(before[:, 1 - j, :], before[:, j, :], mask[:, j, :], ALU.add)\
                    .then_inc(s["before_ready"], 1)

            def scatter(b, j):
                pool.wait_ge(s["zeroed"], 16 * (SLOTS // (4 * P)))
                pool.wait_ge(s["n_ready"], b + 1)
                pool.wait_ge(s["sslot_ready"], b + 1)
                for k in range(K):
                    pool.indirect_dma_start(rows_in, bass.IndirectOffsetOnAxis(ap=sslot[:, b % NR, k:k + 1], axis=0),
                                            n_row[:, b % NR, :], None, bounds_check=SLOTS - 1, oob_is_err=False)\
                        .then_inc(scattered[b % NR], 16)

            run([(-1, times_v), (1, norm_scales), (3, scatter), (2, count)])
            for q in range(WB):
                pool.wait_ge(stored[q], 16 * E // WB)
            pool.wait_ge(s["gslot_ready"], B)

            def gather(b, j, first):
                if not first:
                    pool.wait_ge(s["out_free"], b - 1)
                pool.tensor_copy(gslot[:, j, :], gslot_all[:, bass.ds(b * K, K)]).then_inc(s["gslot_set"], 1)
                pool.wait_ge(s["gslot_set"], b + 1)
                pool.sem_inc(s["held_pool"], 1)
                for k in range(K):
                    pool.indirect_dma_start(G[:, j, k, :], None, rows_out,
                                            bass.IndirectOffsetOnAxis(ap=gslot[:, j, k:k + 1], axis=0))\
                        .then_inc(gathered[j], 16)

            gather(0, 0, True)
            gather(1, 1, True)
            with pool.Fori(1, B // 2) as i:
                gather(2 * i, 0, False)
                gather(2 * i + 1, 1, False)

        @block.scalar
        def _(act):
            for m, vec in enumerate((time_decay, time_first, norm_w)):
                act.dma_start(rows6[HC * m:HC * (m + 1), :], vec.rearrange("(h p) -> h p", p=P)).then_inc(s["col_in"], 16)
            act.wait_ge(s["colT_ready"], 1)
            act.activation(cols6[:, :], COLT, ACT.Copy).then_inc(s["cols6_done"], 1)
            act.wait_ge(s["cols6_done"], 1)
            act.activation(etd[:, :], td, ACT.Exp).then_inc(s["decay_e"], 1)
            act.wait_ge(s["decay_e"], 1)
            act.activation(dcol[:, :], etd[:, :], ACT.Exp, scale=-1.0).then_inc(s["cols_done"], 1)
            act.wait_ge(s["tf_clamped"], 1)
            act.activation(ucol[:, :], tfc[:, :], ACT.Exp).then_inc(s["cols_done"], 1)
            act.wait_ge(s["gwT_ready"], 1)
            act.activation(gwT[:, :, :], GWT, ACT.Copy).then_inc(s["gwT_done"], 1)
            act.wait_ge(s["nb1_done"], 1)

            def exp_k(b, j):
                if b >= 2:
                    act.wait_ge(s["xt_ready"], b - 1)
                act.activation(ek[:, j, :], x_all[:, bass.ds(b, 1), :].rearrange("p o c -> p (o c)"), ACT.Exp,
                               bias=nb1[:, bass.ds(b, 1)], scale=rstd1[:, bass.ds(b, 1)]).then_inc(s["ek_ready"], 1)

            def normed(b, j):
                act.wait_ge(s["nb2_done"], b + 1)
                act.wait_ge(s["rs2_done"], 2 * b + 2)
                if b >= NR:
                    act.wait_ge(scattered[b % NR], 16 * K * (b // NR))
                act.activation(n_row[:, b % NR, :], x1[:, j, :], ACT.Identity, bias=nb2[:, j, 1:2],
                               scale=rs2[:, j, 1:2]).then_inc(s["n_ready"], 1)
                act.activation(base_all[:, bass.ds(b, 1), :].rearrange("p o c -> p (o c)"), x1[:, j, :], ACT.Identity,
                               bias=nb2[:, j, 0:1], scale=rs2[:, j, 2:3]).then_inc(s["base_ready"], 1)

            def normed_T(b, j):
                act.wait_ge(s["nt_ready"], b + 1)
                if b >= 2:
                    act.wait_ge(s["lg_ready"], b - 1)
                for h in range(HC):
                    act.activation(hT[:, j, h, :], NT[j][:, h, :], ACT.Copy, scale=nw[:, h:h + 1]).then_inc(s["hT_ready"], 1)
                for h in range(HC):
                    act.activation(hT_all[:, h, bass.ds(b, 1), :].rearrange("p o t -> p (o t)"), NT[j][:, h, :],
                                   ACT.Copy, scale=nw[:, h:h + 1]).then_inc(s["hTall_done"], 1)

            def pick_weights(b, j):
                act.wait_ge(s["top_ready"], b + 1)
                act.activation(nmax[:, j, :], top8[:, j, 0:1], ACT.Copy, scale=-1.0).then_inc(s["nmax_done"], 1)
                act.wait_ge(s["nmax_done"], b + 1)
                if b >= 2:
                    act.wait_ge(s["w_done"], b - 1)
                act.activation(ew[:, j, :], top8[:, j, 0:K], ACT.Exp, bias=nmax[:, j, :],
                               accum_out=esum[:, j, :]).then_inc(s["ew_ready"], 1)

            run([(-2, exp_k), (1, normed), (1, normed_T), (2, pick_weights)])

            def sh_silu(c, j):
                act.wait_ge(s["sh_g"], c + 1)
                if c >= 2:
                    act.wait_ge(s["sh_a"], c - 1)
                act.activation(sg[:, j, :], FG[j][:, 0, :], ACT.Silu).then_inc(s["sh_s"], 1)

            for c in range(B // 2):
                sh_silu(c, c % 2)
            act.wait_ge(s["sh_a"], B // 2)

            def rows_to_sbuf(e, j):
                act.wait_ge(s["f_xt"], e + 1)
                act.wait_ge(s["f_g"], e - 1) if not isinstance(e, int) or e >= 2 else None
                for h in range(HC):
                    act.activation(xT[:, j, h, :], FX[j][:, h, :], ACT.Copy, scale=nw[:, h:h + 1]).then_inc(s["f_x"], 1)

            def silu(e, j):
                act.wait_ge(s["f_g"], e + 1)
                act.wait_ge(s["f_a"], e - 1) if not isinstance(e, int) or e >= 2 else None
                act.activation(sg[:, j, :], FG[j][:, 0, :], ACT.Silu).then_inc(s["f_s"], 1)

            rows_to_sbuf(0, 0)
            for e in range(WB):
                rows_to_sbuf(e + 1, (e + 1) % 2)
                silu(e, e % 2)
            with act.Fori(1, E // WB - 1) as i:
                for q in range(WB):
                    rows_to_sbuf(WB * i + q + 1, (q + 1) % 2)
                    silu(WB * i + q, q % 2)
            for e in range(E - WB, E):
                if e < E - 1:
                    rows_to_sbuf(e + 1, (e + 1) % 2)
                silu(e, e % 2)

        @block.vector
        def _(dve):
            dve.wait_ge(s["cols6_done"], 1)
            dve.tensor_scalar(tfc[:, :], tf, U_MAX, -U_MAX, ALU.min, ALU.max).then_inc(s["tf_clamped"], 1)
            dve.wait_ge(s["cols_done"], 1)
            for h in range(HC):
                dve.tensor_copy(decay[:, :, h, 1:T], dcol[:, h:h + 1].rearrange("p (a b) -> p a b", a=1)
                                .to_broadcast([P, 2, T - 1])).then_inc(s["decay_done"], 1)
            dve.memset(decay[:, :, :, 0:1], 0.0).then_inc(s["decay_done"], 1)
            dve.wait_ge(s["x0_in"], 16)
            dve.wait_ge(s["x1_in"], 16)
            with dve.Fori(0, B) as b:
                dve.bn_stats(st1[:, bass.ds(b, 1), :].rearrange("p o c -> p (o c)"),
                             x_all[:, bass.ds(b, 1), :].rearrange("p o c -> p (o c)")).then_inc(s["st1_done"], 1)
            dve.wait_ge(s["st1_done"], B)
            for b in range(B):
                dve.bn_aggr(mv1[:, b, :], st1[:, b, :]).then_inc(s["mv1_done"], 1)
            dve.wait_ge(s["mv1_done"], B)
            dve.wait_ge(s["rstd1_done"], 1)
            dve.scalar_tensor_tensor(out=nb1[:, :], in0=mv1[:, :, 0], scalar=-1.0, in1=rstd1[:, :],
                                     op0=ALU.mult, op1=ALU.mult).then_inc(s["nb1_done"], 1)
            dve.wait_ge(s["decay_done"], HC + 1)
            dve.wait_ge(s["cols_done"], 2)
            dve.wait_ge(s["consts"], 4)

            def wkv(b, j):
                later = b >= 2
                dve.wait_ge(s["xt_ready"], b + 1)
                if later:
                    dve.wait_ge(s["nd_done"], 2 * b - 2)
                dve.tensor_tensor_scan(S[:, j].rearrange("p a h t -> p (a h t)"),
                                       decay[:, :, :, :].rearrange("p a h t -> p (a h t)"),
                                       XT[j].rearrange("p a h t -> p (a h t)"), 0.0, ALU.mult, ALU.add)\
                    .then_inc(s["scan_done"], 1)
                dve.wait_ge(s["scan_done"], b + 1)
                if later:
                    dve.wait_ge(s["y_ready"], b - 1)
                dve.tensor_copy(ND[:, j, :, :, 0], XT[j][:, :, :, 0]).then_inc(s["col0_done"], 1)
                for h in range(HC):
                    dve.scalar_tensor_tensor(out=ND[:, j, :, h, 1:T], in0=XT[j][:, :, h, 1:T], scalar=ucol[:, h:h + 1],
                                             in1=S[:, j, :, h, 0:T - 1], op0=ALU.mult, op1=ALU.add)\
                        .then_inc(s["nd_done"], 1)
                dve.wait_ge(s["nd_done"], 2 * b + 2)
                dve.wait_ge(s["col0_done"], b + 1)
                dve.reciprocal(R[:, j], ND[:, j, 0]).then_inc(s["recip_done"], 1)
                dve.wait_ge(s["recip_done"], b + 1)
                if later:
                    dve.wait_ge(s["yt_ready"], b - 1)
                dve.tensor_tensor(Y[:, j], ND[:, j, 1], R[:, j], ALU.mult).then_inc(s["y_ready"], 1)

            def residual(b, j):
                later = b >= 2
                dve.wait_ge(s["yt_ready"], b + 1)
                if later:
                    dve.wait_ge(s["base_ready"], b - 1)
                dve.tensor_tensor(x1[:, j, :], YT[j], x_all[:, bass.ds(b, 1), :].rearrange("p o c -> p (o c)"),
                                  ALU.add).then_inc(s["x1_ready"], 1)
                dve.wait_ge(s["x1_ready"], b + 1)
                dve.bn_stats(st2[:, j, :], x1[:, j, :]).then_inc(s["st2_done"], 1)
                dve.wait_ge(s["st2_done"], b + 1)
                if later:
                    dve.wait_ge(s["nb2_done"], b - 1)
                dve.bn_aggr(mv2[:, j, :], st2[:, j, :]).then_inc(s["mv2_done"], 1)

            def pick(b, j):
                later = b >= 2
                dve.wait_ge(s["lg_ready"], b + 1)
                if later:
                    dve.wait_ge(s["ew_ready"], b - 1)
                dve.max(top8[:, j, :], LG).then_inc(s["top_ready"], 1)
                dve.wait_ge(s["top_ready"], b + 1)
                dve.max_index(idx8[:, j, :], top8[:, j, :], LG).then_inc(s["idx_done"], 1)
                dve.wait_ge(s["idx_done"], b + 1)
                dve.tensor_copy(idxf[:, j, :], idx8[:, j, 0:K]).then_inc(s["idxf_done"], 1)
                dve.wait_ge(s["idxf_done"], b + 1)
                dve.tensor_tensor(onehot[:, j, :, :], iota_e[:, :].unsqueeze(1).to_broadcast([P, K, E]),
                                  idxf[:, j, :].unsqueeze(2).to_broadcast([P, K, E]), ALU.is_equal)\
                    .then_inc(s["onehot_done"], 1)
                dve.wait_ge(s["onehot_done"], b + 1)
                if later:
                    dve.wait_ge(s["before_ready"], b)
                    dve.wait_ge(s["pos_ready"], b - 1)
                with nc.allow_low_precision("zeros and ones"):
                    dve.tensor_reduce(mask[:, j, :], onehot[:, j, :, :].rearrange("p k e -> p e k"), AX.X, ALU.add)\
                        .then_inc(s["mask_ready"], 1)

            def slot_numbers(b, j):
                later = b >= 2
                dve.wait_ge(s["pos_ready"], b + 1)
                dve.scalar_tensor_tensor(out=slots[:, j, 0, :], in0=PO, scalar=float(CAP - 1), in1=slot0[:, :],
                                         op0=ALU.min, op1=ALU.add).then_inc(s["ga_done"], 1)
                dve.tensor_scalar(over[:, j, :], PO, float(CAP), float(OVER), ALU.is_ge, ALU.mult)\
                    .then_inc(s["over_done"], 1)
                dve.wait_ge(s["ga_done"], b + 1)
                dve.wait_ge(s["over_done"], b + 1)
                dve.tensor_tensor(slots[:, j, 1, :], slots[:, j, 0, :], over[:, j, :], ALU.add)\
                    .then_inc(s["slots_done"], 1)
                dve.wait_ge(s["slots_done"], b + 1)
                dve.tensor_tensor(picked[:, j], onehot[:, j, :, :].unsqueeze(1).to_broadcast([P, 2, K, E]),
                                  slots[:, j].unsqueeze(2).to_broadcast([P, 2, K, E]), ALU.mult)\
                    .then_inc(s["picked_done"], 1)
                dve.wait_ge(s["picked_done"], b + 1)
                dve.tensor_reduce(slotf[:, j], picked[:, j], AX.X, ALU.add).then_inc(s["slotf_done"], 1)
                dve.wait_ge(s["slotf_done"], b + 1)
                if b >= NR:
                    dve.wait_ge(scattered[b % NR], 16 * K * (b // NR))
                dve.tensor_copy(sslot[:, b % NR, :], slotf[:, j, 1, :]).then_inc(s["sslot_ready"], 1)
                dve.tensor_copy(gslot_all[:, bass.ds(b * K, K)], slotf[:, j, 0, :])\
                    .then_inc(s["gslot_ready"], 1)
                dve.wait_ge(s["ew_ready"], b + 1)
                dve.reciprocal(rsum[:, j, :], esum[:, j, :]).then_inc(s["rsum_done"], 1)
                dve.wait_ge(s["rsum_done"], b + 1)
                dve.tensor_scalar(w_all[:, bass.ds(b, 1), :].rearrange("p o k -> p (o k)"), ew[:, j, :], rsum[:, j, :], None,
                                  ALU.mult).then_inc(s["w_done"], 1)

            run([(0, wkv), (3, slot_numbers), (1, residual), (2, pick)])

            for c in range(B // 2 + 1):
                if c < B // 2:
                    dve.wait_ge(s["sh_s"], c + 1)
                    if c >= 2:
                        dve.wait_ge(s["sh_y"], c - 1)
                    dve.tensor_tensor(act_t[:, c % 2, :], sg[:, c % 2, :], FG[c % 2][:, 1, :], ALU.mult)\
                        .then_inc(s["sh_a"], 1)
                if c >= 1:
                    d = c - 1
                    dve.wait_ge(s["sh_y"], d + 1)
                    dve.wait_ge(s["base_ready"], 2 * d + 2)
                    dve.tensor_tensor(base_all[:, 2 * d:2 * d + 2, :], base_all[:, 2 * d:2 * d + 2, :], FY[d % 2],
                                      ALU.add).then_inc(s["sh_b"], 1)

            def gated(e, j):
                dve.wait_ge(s["f_s"], e + 1)
                dve.wait_ge(s["f_y"], e - 1) if not isinstance(e, int) or e >= 2 else None
                dve.tensor_tensor(act_t[:, j, :], sg[:, j, :], FG[j][:, 1, :], ALU.mult).then_inc(s["f_a"], 1)

            def rows_out_to_sbuf(e, q, n):
                dve.wait_ge(s["f_y"], e + 1)
                if not isinstance(e, int) or e >= WB:
                    dve.wait_ge(stored[q], 16 * n)
                dve.tensor_copy(yo[:, q, :, :], FY[q % 2]).then_inc(s["f_yo"], 1)

            for e in range(WB):
                gated(e, e % 2)
                if e:
                    rows_out_to_sbuf(e - 1, e - 1, 0)
            with dve.Fori(1, E // WB - 1) as i:
                for q in range(WB):
                    gated(WB * i + q, q % 2)
                    rows_out_to_sbuf(WB * i + q - 1, (q - 1) % WB, i - (q == 0))
            for e in range(E - WB, E):
                gated(e, e % 2)
                rows_out_to_sbuf(e - 1, (e - 1) % WB, (e - 1) // WB)
            rows_out_to_sbuf(E - 1, WB - 1, E // WB - 1)

            dve.wait_ge(s["sh_b"], B // 2)
            dve.wait_ge(s["w_done"], B)

            def combine(b, j, n):
                dve.wait_ge(gathered[j], 16 * K * (n + 1))
                for k in range(K):
                    src = base_all[:, bass.ds(b, 1), :].rearrange("p o c -> p (o c)") if k == 0 else part[:, j, k - 1, :]
                    dst = res[:, j, :] if k == K - 1 else part[:, j, k, :]
                    if k:
                        dve.wait_ge(s["tail_part"], (K - 1) * b + k)
                    if k == K - 1 and not (isinstance(b, int) and b < 2):
                        dve.wait_ge(out_done[j], 16 * n)
                    done = dve.scalar_tensor_tensor(out=dst, in0=G[:, j, k, :],
                                                    scalar=w_all[:, bass.ds(b, 1), k], in1=src,
                                                    op0=ALU.mult, op1=ALU.add)
                    if k < K - 1:
                        done.then_inc(s["tail_part"], 1)
                    else:
                        done.then_inc(s["res_ready"], 1)
                dve.wait_ge(s["res_ready"], b + 1)
                dve.sem_inc(s["out_free"], 1)

            combine(0, 0, 0)
            combine(1, 1, 0)
            with dve.Fori(1, B // 2) as i:
                combine(2 * i, 0, i)
                combine(2 * i + 1, 1, i)

        @block.tensor
        def _(pe):
            pe.wait_ge(s["ident_set"], 2)
            pe.wait_ge(s["col_in"], 48)
            nc.tensor.transpose(COLT, rows6[:, :], ident[0:3 * HC, 0:3 * HC]).then_inc(s["colT_ready"], 1)
            pe.wait_ge(s["gw_in"], 16)
            for h in range(HC):
                last = nc.tensor.transpose(GWT[:, h, :], gw[:, h * P:(h + 1) * P], ident[0:E, 0:E])
            last.then_inc(s["gwT_ready"], 1)
            pe.wait_ge(s["gwT_done"], 1)
            pe.wait_ge(s["tri_set"], 2)
            pe.wait_ge(s["consts"], 4)

            def to_channels(b, j):
                pe.wait_ge(s["ekv_ready"], b + 1)
                if b >= 2:
                    pe.wait_ge(s["nd_done"], 2 * b - 2)
                    pe.wait_ge(s["col0_done"], b - 1)
                for a, src in enumerate((ek, ekv)):
                    for h in range(HC):
                        last = nc.tensor.transpose(XT[j][:, a, h, :], src[:, j, h * P:(h + 1) * P], ident[:, :])
                last.then_inc(s["xt_ready"], 1)

            def to_tokens(b, j):
                pe.wait_ge(s["y_ready"], b + 1)
                if b >= 2:
                    pe.wait_ge(s["x1_ready"], b - 1)
                for h in range(HC):
                    last = nc.tensor.transpose(YT[j][:, h * P:(h + 1) * P], Y[:, j, h, :], ident[:, :])
                last.then_inc(s["yt_ready"], 1)

            def normed_to_channels(b, j):
                pe.wait_ge(s["n_ready"], b + 1)
                if b >= 2:
                    pe.wait_ge(s["hTall_done"], HC * (b - 1))
                for h in range(HC):
                    last = nc.tensor.transpose(NT[j][:, h, :], n_row[:, b % NR, h * P:(h + 1) * P], ident[:, :])
                last.then_inc(s["nt_ready"], 1)

            def logits(b, j):
                pe.wait_ge(s["hT_ready"], HC * (b + 1))
                if b >= 1:
                    pe.wait_ge(s["idx_done"], b)
                for h in range(HC):
                    last = nc.tensor.matmul(LG, hT[:, j, h, :], gwT[:, h, :], start=(h == 0), stop=(h == HC - 1))
                last.then_inc(s["lg_ready"], 1)

            def positions(b, j):
                pe.wait_ge(s["mask_ready"], b + 1)
                pe.wait_ge(s["before_ready"], b + 1)
                if b >= 1:
                    pe.wait_ge(s["over_done"], b)
                    pe.wait_ge(s["ga_done"], b)
                nc.tensor.matmul(PO, tri[:, :], mask[:, j, :], start=True, stop=False)
                nc.tensor.matmul(PO, ones[:, :], before[:, j, :], start=False, stop=True).then_inc(s["pos_ready"], 1)

            run([(-1, to_channels), (0, to_tokens), (1, normed_to_channels), (1, logits), (2, positions)])

            pe.wait_ge(s["sh_in"], 48)
            pe.wait_ge(s["hTall_done"], HC * B)
            pe.wait_ge(s["x1_ready"], B)
            for c in range(B // 2 + 1):
                if c < B // 2:
                    if c >= 2:
                        pe.wait_ge(s["sh_a"], c - 1)
                    for a in range(2):
                        for h in range(HC):
                            last = nc.tensor.matmul(FG[c % 2][:, a, :], sgu[:, h, a, :],
                                                    hT_all[:, h, 2 * c:2 * c + 2, :].rearrange("p b t -> p (b t)"),
                                                    start=(h == 0), stop=(h == HC - 1))
                    last.then_inc(s["sh_g"], 1)
                if c >= 1:
                    d = c - 1
                    pe.wait_ge(s["sh_a"], d + 1)
                    if d >= 2:
                        pe.wait_ge(s["sh_b"], d - 1)
                    for a in range(2):
                        last = nc.tensor.matmul(FY[d % 2][:, a, :], act_t[:, d % 2, a * P:(a + 1) * P], sdn[:, :],
                                                start=True, stop=True)
                    last.then_inc(s["sh_y"], 1)
            pe.wait_ge(s["sh_b"], B // 2)
            pe.wait_ge(s["nd_done"], 2 * B)

            def rows_to_channels(e, q, n):
                pe.wait_ge(xg_in[q], 16 * (n + 1))
                if not isinstance(e, int) or e >= 2:
                    pe.wait_ge(s["f_x"], 2 * e - 2)
                for h in range(HC):
                    for a in range(2):
                        last = nc.tensor.transpose(FX[q % 2][:, h, a * P:(a + 1) * P], xg[q][:, a, h * P:(h + 1) * P],
                                                   ident[:, :])
                last.then_inc(s["f_xt"], 1)

            def gate_up(e, q, n):
                pe.wait_ge(w_in[q], 32 * (n + 1))
                pe.wait_ge(s["f_x"], 2 * e + 2)
                if not isinstance(e, int) or e >= 2:
                    pe.wait_ge(s["f_a"], e - 1)
                for a in range(2):
                    for h in range(HC):
                        last = nc.tensor.matmul(FG[q % 2][:, a, :], w13b[q][:, h, a, :], xT[:, q % 2, h, :],
                                                start=(h == 0), stop=(h == HC - 1))
                last.then_inc(s["f_g"], 1)

            def down(e, q):
                pe.wait_ge(s["f_a"], e + 1)
                if not isinstance(e, int) or e >= 2:
                    pe.wait_ge(s["f_yo"], e - 1)
                for a in range(2):
                    last = nc.tensor.matmul(FY[q % 2][:, a, :], act_t[:, q % 2, a * P:(a + 1) * P], w2b[q][:, :],
                                            start=True, stop=True)
                last.then_inc(s["f_y"], 1)

            rows_to_channels(0, 0, 0)
            for e in range(WB):
                rows_to_channels(e + 1, (e + 1) % WB, (e + 1) // WB)
                gate_up(e, e, 0)
                if e:
                    down(e - 1, e - 1)
            with pe.Fori(1, E // WB - 1) as i:
                for q in range(WB):
                    rows_to_channels(WB * i + q + 1, (q + 1) % WB, i + (q == WB - 1))
                    gate_up(WB * i + q, q, i)
                    down(WB * i + q - 1, (q - 1) % WB)
            for e in range(E - WB, E):
                if e < E - 1:
                    rows_to_channels(e + 1, (e + 1) % WB, (e + 1) // WB)
                gate_up(e, e % WB, e // WB)
                down(e - 1, (e - 1) % WB)
            down(E - 1, WB - 1)


_INS = ['x', 'ctx_2048', 'L0_xattn_time_decay', 'L0_xattn_time_first', 'L0_ffn_norm_w', 'L0_ffn_gate_w',
        'L0_ffn_w13', 'L0_ffn_w2', 'L0_ffn_shared_gate_w', 'L0_ffn_shared_up_w', 'L0_ffn_shared_down_w']


def kernel(**inputs):
    import numpy as _np
    import concourse.bacc as _bacc
    from concourse import mybir as _mybir
    from concourse.bass_utils import run_bass_kernel_spmd as _run

    nc = _bacc.Bacc("TRN2", target_bir_lowering=False, num_devices=1)
    arrays, args = {}, []
    for name in _INS:
        a = _np.ascontiguousarray(inputs[name])
        arrays[f"in_{name}_dram"] = a
        args.append(nc.dram_tensor(f"in_{name}_dram", a.shape, _mybir.dt.from_np(a.dtype), kind="ExternalInput").ap())
    args.append(nc.dram_tensor("out_dram", (B, T, C), _mybir.dt.float32, kind="ExternalOutput").ap())
    xattn_moe(nc, *args)
    r = _run(nc, [arrays], core_ids=[0])
    return r.results[0]["out_dram"]
```

```python
import concourse.bass as bass
from concourse import mybir
from contextlib import ExitStack

F32 = mybir.dt.float32
BF16 = mybir.dt.bfloat16
I32 = mybir.dt.int32
U32 = mybir.dt.uint32
ALU = mybir.AluOpType
ACT = mybir.ActivationFunctionType
AX = mybir.AxisListType

P = 128
B, T, C = 8, 128, 256
E, K, F = 32, 4, 128
CAP = 2 * B * T * K // E
HC = C // P
SLOTS = E * CAP
LN_EPS, RMS_EPS = 1e-5, 1e-6
PICKS = B * T * K
RW = C + 2 * K
OUTSIDE = 16384
U_MAX = 60.0
NR = 4
GB = 4
WB = 4


def xattn_moe(nc, x, ctx_in, time_decay, time_first, norm_w, gate_w, w13, w2, sh_gate, sh_up, sh_down, out):
    ctx = ExitStack()
    with ctx:
        def sb(name, shape, dt=F32):
            return ctx.enter_context(nc.sbuf_tensor(name, shape, dt))

        def sem(name):
            return ctx.enter_context(nc.semaphore(name))

        rows_in = nc.dram_tensor("rows_in", (SLOTS, RW), F32, kind="Internal").ap()
        rows_out = nc.dram_tensor("rows_out", (PICKS, C), F32, kind="Internal").ap()
        last_rows = nc.dram_tensor("last_rows", (E, C), F32, kind="Internal").ap()

        x_all = sb("x_all", [P, B, C])
        v_all = sb("v_all", [P, B, C])
        base_all = sb("base_all", [P, B, C])
        hT_all = sb("hT_all", [P, HC, B, T])
        w_all = sb("w_all", [P, B, K])
        slot_all = sb("slot_all", [P, B, K])
        expert_all = sb("expert_all", [P, B, K])
        pick_no = sb("pick_no", [P, B, K])
        fits = sb("fits", [P, B, K])
        last_all = sb("last_all", [P, B * K], I32)
        slot_max = sb("slot_max", [P, 1])
        slot_top = sb("slot_top", [P, 1])
        overflow = sb("overflow", [P, 1], I32)

        ident = sb("ident", [P, P])
        tri = sb("tri", [P, P], BF16)
        ones = sb("ones", [P, P], BF16)
        iota_e = sb("iota_e", [P, E])
        slot0 = sb("slot0", [P, E])
        rows6 = sb("rows6", [3 * HC, P])
        cols6 = sb("cols6", [P, 3 * HC])
        td, tf, nw = (cols6[:, HC * m:HC * (m + 1)] for m in range(3))
        etd = sb("etd", [P, HC])
        dcol = sb("dcol", [P, HC])
        ucol = sb("ucol", [P, HC])
        tfc = sb("tfc", [P, HC])
        decay = sb("decay", [P, 2, HC, T])
        gw = sb("gw", [E, C])
        gwT = sb("gwT", [P, HC, E])
        sgu = sb("sgu", [P, HC, 2, F])
        sdn = sb("sdn", [P, C])
        zeros = sb("zeros", [P, 4 * RW])
        neg_half = sb("neg_half", [P, B])

        st1 = sb("st1", [P, B, 6])
        mv1 = sb("mv1", [P, B, 2])
        ve1 = sb("ve1", [P, B])
        rstd1 = sb("rstd1", [P, B])
        nb1 = sb("nb1", [P, B])

        ek = sb("ek", [P, 2, C])
        ekv = sb("ekv", [P, 2, C])
        S = sb("S", [P, 2, 2, HC, T])
        ND = sb("ND", [P, 2, 2, HC, T])
        R = sb("R", [P, 2, HC, T])
        Y = sb("Y", [P, 2, HC, T])
        x1 = sb("x1", [P, 2, C])
        st2 = sb("st2", [P, 2, 6])
        mv2 = sb("mv2", [P, 2, 2])
        ve2 = sb("ve2", [P, 2, 2])
        rs2 = sb("rs2", [P, 2, 3])
        mr2 = sb("mr2", [P, 2, 2])
        nb2 = sb("nb2", [P, 2, 2])
        n_row = sb("n_row", [P, NR, RW])
        hT = sb("hT", [P, 2, HC, T])
        top8 = sb("top8", [P, 2, 8])
        idx8 = sb("idx8", [P, 2, 8], U32)
        nmax = sb("nmax", [P, 2, 1])
        ew = sb("ew", [P, 2, K])
        esum = sb("esum", [P, 2, 1])
        rsum = sb("rsum", [P, 2, 1])
        onehot = sb("onehot", [P, 2, K, E])
        mask = sb("mask", [P, 2, E], BF16)
        before = sb("before", [P, 2, E], BF16)
        slots = sb("slots", [P, 2, 2, E])
        over = sb("over", [P, 2, E])
        picked = sb("picked", [P, 2, K, E])
        last_idx = sb("last_idx", [P, 2, K], I32)
        sslot = sb("sslot", [P, NR, K], I32)

        w13b = [sb(f"w13b{q}", [P, HC, 2, F]) for q in range(WB)]
        w2b = [sb(f"w2b{q}", [P, C]) for q in range(WB)]
        xg = [sb(f"xg{q}", [P, 2, RW]) for q in range(WB)]
        own = sb("own", [P, WB, 2, K])
        owned = sb("owned", [P, WB, 2])
        pick_idx = sb("pick_idx", [P, WB, 2], I32)
        xT = sb("xT", [P, 2, HC, CAP])
        sg = sb("sg", [P, 2, CAP])
        act_t = sb("act_t", [P, 2, CAP])
        yo = sb("yo", [P, WB, 2, C])
        G = sb("G", [P, GB, K, C])
        res = sb("res", [P, 2, C])
        part = sb("part", [P, 2, K, C])

        bank = [ctx.enter_context(nc.psum_tensor(f"bank{i}", [P, 512], F32)) for i in range(8)]
        XT = [bank[j][:, :].rearrange("p (a h t) -> p a h t", a=2, h=HC) for j in range(2)]
        YT = [bank[2 + j][:, 0:C] for j in range(2)]
        NT = [bank[4 + j][:, 0:C].rearrange("p (h t) -> p h t", h=HC) for j in range(2)]
        LG = bank[6][:, 0:E]
        PO = bank[7][:, 0:E]
        GWT = bank[6][:, 256:256 + HC * E].rearrange("p (h e) -> p h e", h=HC)
        COLT = bank[7][:, 256:256 + 3 * HC]
        FX = [bank[j][:, :].rearrange("p (h s) -> p h s", h=HC) for j in range(2)]
        FG = [bank[2 + j][:, :].rearrange("p (a s) -> p a s", a=2) for j in range(2)]
        FY = [bank[4 + j][:, :].rearrange("p (a c) -> p a c", a=2) for j in range(2)]

        names = """held_pool colT_ready cols6_done x0_in x1_in v0_in v1_in col_in gw_in sh_in zero_set zeroed consts ident_set tri_set
            st1_done mv1_done ve1_done rstd1_done nb1_done decay_e tf_clamped cols_done decay_done gwT_ready gwT_done
            ek_ready ekv_ready xt_ready col0_done scan_done nd_done recip_done y_ready yt_ready x1_ready st2_done
            mv2_done ve2_done rs2_done mr2_done nb2_done n_ready base_ready nt_ready hT_ready hTall_done lg_ready
            top_ready idx_done expert_ready expert_all_done nmax_done ew_ready rsum_done w_done onehot_done mask_ready before_ready
            pos_ready ga_done over_done slots_done picked_done slot_ready sslot_ready own_done owned_done pick_ready fits_done last_all_done last_set slot_max_done slot_top_done overflow_done fixed pickno_ready
            sh_g sh_s sh_a sh_y sh_b f_xt f_x f_g f_s f_a f_y f_yo tail_part out_free res_ready""".split()
        s = {n: sem(n) for n in names}
        scattered = [sem(f"scattered{r}") for r in range(NR)]
        w_in = [sem(f"w_in{q}") for q in range(WB)]
        xg_in = [sem(f"xg_in{q}") for q in range(WB)]
        row_out = [sem(f"row_out{q}") for q in range(WB)]
        gathered = [sem(f"gathered{g}") for g in range(GB)]
        last_stored = [sem(f"last_stored{q}") for q in range(WB)]
        last_in = sem("last_in")
        out_done = [sem(f"out_done{j}") for j in range(2)]

        def run(stages):
            for n in range(min(lag for lag, _ in stages), B + max(lag for lag, _ in stages)):
                for lag, stage in stages:
                    if 0 <= n - lag < B:
                        stage(n - lag, (n - lag) % 2)

        block = ctx.enter_context(nc.Block())

        @block.sync
        def _(sp):
            xv = x.rearrange("b t c -> t b c")
            vv = ctx_in.rearrange("b t c -> t b c")
            h = B // 2
            sp.dma_start(x_all[:, 0:h, :], xv[:, 0:h, :]).then_inc(s["x0_in"], 16)
            sp.dma_start(x_all[:, h:B, :], xv[:, h:B, :]).then_inc(s["x1_in"], 16)
            sp.dma_start(v_all[:, 0:h, :], vv[:, 0:h, :]).then_inc(s["v0_in"], 16)
            sp.dma_start(v_all[:, h:B, :], vv[:, h:B, :]).then_inc(s["v1_in"], 16)
            sp.dma_start(gw[:, :], gate_w).then_inc(s["gw_in"], 16)
            sp.dma_start(sgu[:, :, 0, :], sh_gate.rearrange("(h p) f -> p h f", p=P)).then_inc(s["sh_in"], 16)
            sp.dma_start(sgu[:, :, 1, :], sh_up.rearrange("(h p) f -> p h f", p=P)).then_inc(s["sh_in"], 16)
            sp.dma_start(sdn[:, :], sh_down).then_inc(s["sh_in"], 16)
            sp.wait_ge(s["zero_set"], 1)
            zv = rows_in.rearrange("(a p r) c -> a p (r c)", p=P, r=4)
            for a in range(SLOTS // (4 * P)):
                sp.dma_start(zv[a], zeros[:, :]).then_inc(s["zeroed"], 16)

            def load_weights(e, q):
                sp.dma_start(w13b[q][:, :, :, :].rearrange("p h a f -> p h (a f)"),
                             w13[bass.ds(e, 1)].rearrange("o (h p) f -> p (o h) f", p=P)).then_inc(w_in[q], 16)
                sp.dma_start(w2b[q][:, :], w2[bass.ds(e, 1)].rearrange("o p c -> p (o c)")).then_inc(w_in[q], 16)

            def load_rows(e, q):
                sp.dma_start(xg[q][:, :, :],
                             rows_in[bass.ds(e * CAP, CAP), :].rearrange("(a p) c -> p a c", p=P)).then_inc(xg_in[q], 16)

            def store_last(e, q):
                sp.wait_ge(s["f_yo"], e + 1)
                sp.dma_start(last_rows[bass.ds(e, 1), :], yo[P - 1:P, q, 1, :]).then_inc(last_stored[q], 16)

            for q in range(WB):
                load_weights(q, q)
            for r in range(NR):
                sp.wait_ge(scattered[r], 16 * K * B // NR)
            for q in range(WB):
                load_rows(q, q)

            def refill(e, q, n, first=False):
                sp.wait_ge(s["f_xt"], e + 1)
                sp.wait_ge(s["own_done"], e + 1)
                load_rows(e + WB, q)
                if not first:
                    sp.wait_ge(s["f_y"], e)
                    load_weights(e - 1 + WB, (q - 1) % WB)
                    store_last(e - 1, (q - 1) % WB)

            for q in range(WB):
                refill(q, q, 0, q == 0)
            with sp.Fori(1, E // WB - 1) as i:
                for q in range(WB):
                    refill(WB * i + q, q, i)
            sp.wait_ge(s["f_y"], E - WB)
            load_weights(E - 1, WB - 1)
            for e in range(E - WB - 1, E):
                store_last(e, e % WB)
            ov = out.rearrange("b t c -> t b c")
            for q in range(WB):
                sp.wait_ge(row_out[q], 32 * E // WB)

            def load_picks(b):
                if b >= GB:
                    sp.wait_ge(s["res_ready"], b - GB + 1)
                sp.dma_start(G[:, b % GB], rows_out[b * T * K:(b + 1) * T * K, :].rearrange("(p k) c -> p k c", k=K))\
                    .then_inc(gathered[b % GB], 16)

            for b in range(GB):
                load_picks(b)
            for b in range(B):
                sp.wait_ge(s["res_ready"], b + 1)
                sp.dma_start(ov[:, b:b + 1, :], res[:, b % 2:b % 2 + 1, :]).then_inc(out_done[b % 2], 16)
                if b + GB < B:
                    load_picks(b + GB)
            for j in range(2):
                sp.wait_ge(out_done[j], 16 * B // 2)

        @block.gpsimd
        def _(pool):
            pool.memset(zeros[:, :], 0.0).then_inc(s["zero_set"], 1)
            pool.memset(ident[:, :], 0.0).then_inc(s["ident_set"], 1)
            pool.memset(tri[:, :], 1.0).then_inc(s["tri_set"], 1)
            pool.memset(ones[:, :], 1.0).then_inc(s["consts"], 1)
            pool.memset(neg_half[:, :], -0.5).then_inc(s["consts"], 1)
            pool.memset(before[:, 0, :], 0.0).then_inc(s["before_ready"], 1)
            pool.iota(iota_e[:, :], [[1, E]], base=1, channel_multiplier=0,
                      allow_small_or_imprecise_dtypes=True).then_inc(s["consts"], 1)
            pool.iota(slot0[:, :], [[CAP, E]], base=0, channel_multiplier=0,
                      allow_small_or_imprecise_dtypes=True).then_inc(s["consts"], 1)
            pool.iota(pick_no[:, :, :], [[T * K, B], [1, K]], base=-OUTSIDE, channel_multiplier=K,
                      allow_small_or_imprecise_dtypes=True).then_inc(s["pickno_ready"], 1)
            pool.wait_ge(s["ident_set"], 1)
            pool.affine_select(out=ident[:, :], in_=ident[:, :], compare_op=ALU.not_equal, fill=1.0, base=0,
                               pattern=[[-1, P]], channel_multiplier=1).then_inc(s["ident_set"], 1)
            pool.wait_ge(s["tri_set"], 1)
            pool.affine_select(out=tri[:, :], in_=tri[:, :], compare_op=ALU.is_gt, fill=0.0, base=0,
                               pattern=[[1, P]], channel_multiplier=-1).then_inc(s["tri_set"], 1)
            pool.wait_ge(s["mv1_done"], B)
            pool.tensor_scalar(ve1[:, :], mv1[:, :, 1], LN_EPS, 1.0, ALU.add, ALU.mult).then_inc(s["ve1_done"], 1)
            pool.wait_ge(s["ve1_done"], 1)
            pool.wait_ge(s["consts"], 4)
            pool.tensor_tensor(rstd1[:, :], ve1[:, :], neg_half[:, :], ALU.pow).then_inc(s["rstd1_done"], 1)
            pool.wait_ge(s["v0_in"], 16)
            pool.wait_ge(s["v1_in"], 16)

            def times_v(b, j):
                pool.wait_ge(s["ek_ready"], b + 1)
                pool.tensor_tensor(ekv[:, j, :], ek[:, j, :], v_all[:, bass.ds(b, 1), :].rearrange("p o c -> p (o c)"),
                                   ALU.mult).then_inc(s["ekv_ready"], 1)

            def norm_scales(b, j):
                pool.wait_ge(s["mv2_done"], b + 1)
                pool.tensor_scalar(ve2[:, j, 0:1], mv2[:, j, 1:2], 1.0, LN_EPS, ALU.mult, ALU.add).then_inc(s["ve2_done"], 1)
                pool.tensor_scalar(ve2[:, j, 1:2], mv2[:, j, 1:2], 1.0 + RMS_EPS, LN_EPS * RMS_EPS,
                                   ALU.mult, ALU.add).then_inc(s["ve2_done"], 1)
                pool.wait_ge(s["ve2_done"], 2 * b + 2)
                pool.tensor_tensor(rs2[:, j, 0:2], ve2[:, j, :], neg_half[:, 0:2], ALU.pow).then_inc(s["rs2_done"], 1)
                pool.wait_ge(s["rs2_done"], 2 * b + 1)
                pool.tensor_scalar(rs2[:, j, 2:3], rs2[:, j, 0:1], 1.0, 1.0, ALU.mult, ALU.add).then_inc(s["rs2_done"], 1)
                pool.tensor_scalar(nb2[:, j, :], rs2[:, j, 0:2], mv2[:, j, 0:1], -1.0, ALU.mult, ALU.mult)\
                    .then_inc(s["nb2_done"], 1)

            def count(b, j):
                pool.wait_ge(s["mask_ready"], b + 1)
                pool.wait_ge(s["before_ready"], b + 1)
                pool.wait_ge(s["pos_ready"], b + 1)
                pool.tensor_tensor(before[:, 1 - j, :], before[:, j, :], mask[:, j, :], ALU.add)\
                    .then_inc(s["before_ready"], 1)

            def scatter(b, j):
                pool.wait_ge(s["zeroed"], 16 * (SLOTS // (4 * P)))
                pool.wait_ge(s["n_ready"], b + 1)
                pool.wait_ge(s["pickno_ready"], b + 2)
                pool.wait_ge(s["sslot_ready"], b + 1)
                for k in range(K):
                    pool.indirect_dma_start(rows_in, bass.IndirectOffsetOnAxis(ap=sslot[:, b % NR, k:k + 1], axis=0),
                                            n_row[:, b % NR, :], None, bounds_check=SLOTS - 1, oob_is_err=False)\
                        .then_inc(scattered[b % NR], 16)

            run([(-1, times_v), (1, norm_scales), (3, scatter), (2, count)])

            pool.wait_ge(s["slot_max_done"], 1)
            pool.partition_all_reduce(slot_top[:, :], slot_max[:, :], P, bass.bass_isa.ReduceOp.max).then_inc(s["slot_top_done"], 1)

            def scatter_out(e, q):
                pool.wait_ge(s["pick_ready"], e + 1)
                pool.wait_ge(s["f_yo"], e + 1)
                pool.sem_inc(s["held_pool"], 1)
                for a in range(2):
                    pool.indirect_dma_start(rows_out, bass.IndirectOffsetOnAxis(ap=pick_idx[:, q, a:a + 1], axis=0),
                                            yo[:, q, a, :], None, bounds_check=PICKS - 1, oob_is_err=False)\
                        .then_inc(row_out[q], 16)

            with pool.Fori(0, E // WB) as i:
                for q in range(WB):
                    scatter_out(WB * i + q, q)

            pool.wait_ge(s["overflow_done"], 1)
            pool.wait_ge(s["last_all_done"], 1)
            for q in range(WB):
                pool.wait_ge(last_stored[q], 16 * E // WB)
            flag = pool.value_load(overflow[0:1, 0:1], min_val=0, max_val=1)
            with pool.If(flag == 0):
                pool.sem_inc(s["fixed"], B)
            with pool.If(flag != 0):
                for b in range(B):
                    pool.wait_ge(gathered[b % GB], 16 * (b // GB + 1))
                    if b >= 2:
                        pool.wait_ge(last_in, 16 * K * (b - 1))
                    pool.tensor_copy(last_idx[:, b % 2, :], last_all[:, b * K:(b + 1) * K]).then_inc(s["last_set"], 1)
                    pool.wait_ge(s["last_set"], b + 1)
                    for k in range(K):
                        pool.indirect_dma_start(G[:, b % GB, k, :], None, last_rows,
                                                bass.IndirectOffsetOnAxis(ap=last_idx[:, b % 2, k:k + 1], axis=0),
                                                bounds_check=E - 1, oob_is_err=False).then_inc(last_in, 16)
                    pool.wait_ge(last_in, 16 * K * (b + 1))
                    pool.sem_inc(s["fixed"], 1)

        @block.scalar
        def _(act):
            for m, vec in enumerate((time_decay, time_first, norm_w)):
                act.dma_start(rows6[HC * m:HC * (m + 1), :], vec.rearrange("(h p) -> h p", p=P)).then_inc(s["col_in"], 16)
            act.wait_ge(s["colT_ready"], 1)
            act.activation(cols6[:, :], COLT, ACT.Copy).then_inc(s["cols6_done"], 1)
            act.wait_ge(s["cols6_done"], 1)
            act.activation(etd[:, :], td, ACT.Exp).then_inc(s["decay_e"], 1)
            act.wait_ge(s["decay_e"], 1)
            act.activation(dcol[:, :], etd[:, :], ACT.Exp, scale=-1.0).then_inc(s["cols_done"], 1)
            act.wait_ge(s["tf_clamped"], 1)
            act.activation(ucol[:, :], tfc[:, :], ACT.Exp).then_inc(s["cols_done"], 1)
            act.wait_ge(s["gwT_ready"], 1)
            act.activation(gwT[:, :, :], GWT, ACT.Copy).then_inc(s["gwT_done"], 1)
            act.wait_ge(s["nb1_done"], 1)
            act.wait_ge(s["pickno_ready"], 1)

            def exp_k(b, j):
                if b >= 2:
                    act.wait_ge(s["xt_ready"], b - 1)
                act.activation(ek[:, j, :], x_all[:, bass.ds(b, 1), :].rearrange("p o c -> p (o c)"), ACT.Exp,
                               bias=nb1[:, bass.ds(b, 1)], scale=rstd1[:, bass.ds(b, 1)]).then_inc(s["ek_ready"], 1)

            def normed(b, j):
                act.wait_ge(s["nb2_done"], b + 1)
                act.wait_ge(s["rs2_done"], 2 * b + 2)
                if b >= NR:
                    act.wait_ge(scattered[b % NR], 16 * K * (b // NR))
                act.activation(n_row[:, b % NR, 0:C], x1[:, j, :], ACT.Identity, bias=nb2[:, j, 1:2],
                               scale=rs2[:, j, 1:2]).then_inc(s["n_ready"], 1)
                act.activation(n_row[:, b % NR, C + K:RW], pick_no[:, b, :], ACT.Copy).then_inc(s["pickno_ready"], 1)
                act.activation(base_all[:, bass.ds(b, 1), :].rearrange("p o c -> p (o c)"), x1[:, j, :], ACT.Identity,
                               bias=nb2[:, j, 0:1], scale=rs2[:, j, 2:3]).then_inc(s["base_ready"], 1)

            def normed_T(b, j):
                act.wait_ge(s["nt_ready"], b + 1)
                if b >= 2:
                    act.wait_ge(s["lg_ready"], b - 1)
                for h in range(HC):
                    act.activation(hT[:, j, h, :], NT[j][:, h, :], ACT.Copy, scale=nw[:, h:h + 1]).then_inc(s["hT_ready"], 1)
                for h in range(HC):
                    act.activation(hT_all[:, h, bass.ds(b, 1), :].rearrange("p o t -> p (o t)"), NT[j][:, h, :],
                                   ACT.Copy, scale=nw[:, h:h + 1]).then_inc(s["hTall_done"], 1)

            def pick_weights(b, j):
                act.wait_ge(s["top_ready"], b + 1)
                act.activation(nmax[:, j, :], top8[:, j, 0:1], ACT.Copy, scale=-1.0).then_inc(s["nmax_done"], 1)
                act.wait_ge(s["nmax_done"], b + 1)
                if b >= 2:
                    act.wait_ge(s["w_done"], b - 1)
                act.activation(ew[:, j, :], top8[:, j, 0:K], ACT.Exp, bias=nmax[:, j, :],
                               accum_out=esum[:, j, :]).then_inc(s["ew_ready"], 1)

            run([(-2, exp_k), (1, normed), (1, normed_T), (2, pick_weights)])

            def sh_silu(c, j):
                act.wait_ge(s["sh_g"], c + 1)
                if c >= 2:
                    act.wait_ge(s["sh_a"], c - 1)
                act.activation(sg[:, j, :], FG[j][:, 0, :], ACT.Silu).then_inc(s["sh_s"], 1)

            for c in range(B // 2):
                sh_silu(c, c % 2)
            act.wait_ge(s["sh_a"], B // 2)

            def rows_to_sbuf(e, j):
                act.wait_ge(s["f_xt"], e + 1)
                act.wait_ge(s["f_g"], e - 1) if not isinstance(e, int) or e >= 2 else None
                for h in range(HC):
                    act.activation(xT[:, j, h, :], FX[j][:, h, :], ACT.Copy, scale=nw[:, h:h + 1]).then_inc(s["f_x"], 1)

            def silu(e, j):
                act.wait_ge(s["f_g"], e + 1)
                act.wait_ge(s["f_a"], e - 1) if not isinstance(e, int) or e >= 2 else None
                act.activation(sg[:, j, :], FG[j][:, 0, :], ACT.Silu).then_inc(s["f_s"], 1)

            rows_to_sbuf(0, 0)
            for e in range(WB):
                rows_to_sbuf(e + 1, (e + 1) % 2)
                silu(e, e % 2)
            with act.Fori(1, E // WB - 1) as i:
                for q in range(WB):
                    rows_to_sbuf(WB * i + q + 1, (q + 1) % 2)
                    silu(WB * i + q, q % 2)
            for e in range(E - WB, E):
                if e < E - 1:
                    rows_to_sbuf(e + 1, (e + 1) % 2)
                silu(e, e % 2)

        @block.vector
        def _(dve):
            dve.wait_ge(s["cols6_done"], 1)
            dve.tensor_scalar(tfc[:, :], tf, U_MAX, -U_MAX, ALU.min, ALU.max).then_inc(s["tf_clamped"], 1)
            dve.wait_ge(s["cols_done"], 1)
            for h in range(HC):
                dve.tensor_copy(decay[:, :, h, 1:T], dcol[:, h:h + 1].rearrange("p (a b) -> p a b", a=1)
                                .to_broadcast([P, 2, T - 1])).then_inc(s["decay_done"], 1)
            dve.memset(decay[:, :, :, 0:1], 0.0).then_inc(s["decay_done"], 1)
            dve.wait_ge(s["x0_in"], 16)
            dve.wait_ge(s["x1_in"], 16)
            for b in range(B):
                dve.bn_stats(st1[:, b, :], x_all[:, b, :]).then_inc(s["st1_done"], 1)
            dve.wait_ge(s["st1_done"], B)
            for b in range(B):
                dve.bn_aggr(mv1[:, b, :], st1[:, b, :]).then_inc(s["mv1_done"], 1)
            dve.wait_ge(s["mv1_done"], B)
            dve.wait_ge(s["rstd1_done"], 1)
            dve.scalar_tensor_tensor(out=nb1[:, :], in0=mv1[:, :, 0], scalar=-1.0, in1=rstd1[:, :],
                                     op0=ALU.mult, op1=ALU.mult).then_inc(s["nb1_done"], 1)
            dve.wait_ge(s["decay_done"], HC + 1)
            dve.wait_ge(s["cols_done"], 2)
            dve.wait_ge(s["consts"], 4)

            def wkv(b, j):
                later = b >= 2
                dve.wait_ge(s["xt_ready"], b + 1)
                if later:
                    dve.wait_ge(s["nd_done"], 2 * b - 2)
                dve.tensor_tensor_scan(S[:, j].rearrange("p a h t -> p (a h t)"),
                                       decay[:, :, :, :].rearrange("p a h t -> p (a h t)"),
                                       XT[j].rearrange("p a h t -> p (a h t)"), 0.0, ALU.mult, ALU.add)\
                    .then_inc(s["scan_done"], 1)
                dve.wait_ge(s["scan_done"], b + 1)
                if later:
                    dve.wait_ge(s["y_ready"], b - 1)
                dve.tensor_copy(ND[:, j, :, :, 0], XT[j][:, :, :, 0]).then_inc(s["col0_done"], 1)
                for h in range(HC):
                    dve.scalar_tensor_tensor(out=ND[:, j, :, h, 1:T], in0=XT[j][:, :, h, 1:T], scalar=ucol[:, h:h + 1],
                                             in1=S[:, j, :, h, 0:T - 1], op0=ALU.mult, op1=ALU.add)\
                        .then_inc(s["nd_done"], 1)
                dve.wait_ge(s["nd_done"], 2 * b + 2)
                dve.wait_ge(s["col0_done"], b + 1)
                dve.reciprocal(R[:, j], ND[:, j, 0]).then_inc(s["recip_done"], 1)
                dve.wait_ge(s["recip_done"], b + 1)
                if later:
                    dve.wait_ge(s["yt_ready"], b - 1)
                dve.tensor_tensor(Y[:, j], ND[:, j, 1], R[:, j], ALU.mult).then_inc(s["y_ready"], 1)

            def residual(b, j):
                later = b >= 2
                dve.wait_ge(s["yt_ready"], b + 1)
                if later:
                    dve.wait_ge(s["base_ready"], b - 1)
                dve.tensor_tensor(x1[:, j, :], YT[j], x_all[:, bass.ds(b, 1), :].rearrange("p o c -> p (o c)"),
                                  ALU.add).then_inc(s["x1_ready"], 1)
                dve.wait_ge(s["x1_ready"], b + 1)
                dve.bn_stats(st2[:, j, :], x1[:, j, :]).then_inc(s["st2_done"], 1)
                dve.wait_ge(s["st2_done"], b + 1)
                if later:
                    dve.wait_ge(s["nb2_done"], b - 1)
                dve.bn_aggr(mv2[:, j, :], st2[:, j, :]).then_inc(s["mv2_done"], 1)

            def pick(b, j):
                later = b >= 2
                dve.wait_ge(s["lg_ready"], b + 1)
                if later:
                    dve.wait_ge(s["ew_ready"], b - 1)
                dve.max(top8[:, j, :], LG).then_inc(s["top_ready"], 1)
                dve.wait_ge(s["top_ready"], b + 1)
                dve.max_index(idx8[:, j, :], top8[:, j, :], LG).then_inc(s["idx_done"], 1)
                dve.wait_ge(s["idx_done"], b + 1)
                if b >= NR:
                    dve.wait_ge(scattered[b % NR], 16 * K * (b // NR))
                dve.tensor_scalar(n_row[:, b % NR, C:C + K], idx8[:, j, 0:K], 1.0, None, ALU.add)\
                    .then_inc(s["expert_ready"], 1)
                dve.wait_ge(s["expert_ready"], b + 1)
                dve.tensor_copy(expert_all[:, b, :], n_row[:, b % NR, C:C + K]).then_inc(s["expert_all_done"], 1)
                dve.tensor_tensor(onehot[:, j, :, :], iota_e[:, :].unsqueeze(1).to_broadcast([P, K, E]),
                                  n_row[:, b % NR, C:C + K].unsqueeze(2).to_broadcast([P, K, E]), ALU.is_equal)\
                    .then_inc(s["onehot_done"], 1)
                dve.wait_ge(s["onehot_done"], b + 1)
                if later:
                    dve.wait_ge(s["before_ready"], b)
                    dve.wait_ge(s["pos_ready"], b - 1)
                with nc.allow_low_precision("zeros and ones"):
                    dve.tensor_reduce(mask[:, j, :], onehot[:, j, :, :].rearrange("p k e -> p e k"), AX.X, ALU.add)\
                        .then_inc(s["mask_ready"], 1)

            def slot_numbers(b, j):
                later = b >= 2
                dve.wait_ge(s["pos_ready"], b + 1)
                dve.scalar_tensor_tensor(out=slots[:, j, 0, :], in0=PO, scalar=float(CAP - 1), in1=slot0[:, :],
                                         op0=ALU.min, op1=ALU.add).then_inc(s["ga_done"], 1)
                dve.tensor_scalar(over[:, j, :], PO, float(CAP), float(OUTSIDE), ALU.is_ge, ALU.mult)\
                    .then_inc(s["over_done"], 1)
                dve.wait_ge(s["ga_done"], b + 1)
                dve.wait_ge(s["over_done"], b + 1)
                dve.tensor_tensor(slots[:, j, 1, :], slots[:, j, 0, :], over[:, j, :], ALU.add)\
                    .then_inc(s["slots_done"], 1)
                dve.wait_ge(s["slots_done"], b + 1)
                dve.tensor_tensor(picked[:, j], onehot[:, j, :, :],
                                  slots[:, j, 1, :].unsqueeze(1).to_broadcast([P, K, E]), ALU.mult)\
                    .then_inc(s["picked_done"], 1)
                dve.wait_ge(s["picked_done"], b + 1)
                dve.tensor_reduce(slot_all[:, b, :], picked[:, j], AX.X, ALU.add).then_inc(s["slot_ready"], 1)
                dve.wait_ge(s["slot_ready"], b + 1)
                dve.tensor_copy(sslot[:, b % NR, :], slot_all[:, b, :]).then_inc(s["sslot_ready"], 1)
                dve.wait_ge(s["ew_ready"], b + 1)
                dve.reciprocal(rsum[:, j, :], esum[:, j, :]).then_inc(s["rsum_done"], 1)
                dve.wait_ge(s["rsum_done"], b + 1)
                dve.tensor_scalar(w_all[:, bass.ds(b, 1), :].rearrange("p o k -> p (o k)"), ew[:, j, :], rsum[:, j, :], None,
                                  ALU.mult).then_inc(s["w_done"], 1)

            run([(0, wkv), (3, slot_numbers), (1, residual), (2, pick)])

            for c in range(B // 2 + 1):
                if c < B // 2:
                    dve.wait_ge(s["sh_s"], c + 1)
                    if c >= 2:
                        dve.wait_ge(s["sh_y"], c - 1)
                    dve.tensor_tensor(act_t[:, c % 2, :], sg[:, c % 2, :], FG[c % 2][:, 1, :], ALU.mult)\
                        .then_inc(s["sh_a"], 1)
                if c >= 1:
                    d = c - 1
                    dve.wait_ge(s["sh_y"], d + 1)
                    dve.wait_ge(s["base_ready"], 2 * d + 2)
                    dve.tensor_tensor(base_all[:, 2 * d:2 * d + 2, :], base_all[:, 2 * d:2 * d + 2, :], FY[d % 2],
                                      ALU.add).then_inc(s["sh_b"], 1)

            dve.wait_ge(s["slot_ready"], B)
            dve.wait_ge(s["expert_all_done"], B)
            dve.tensor_reduce(slot_max[:, :], slot_all[:, :, :].rearrange("p b k -> p (b k)"), AX.X, ALU.max)\
                .then_inc(s["slot_max_done"], 1)
            dve.tensor_scalar(fits[:, :, :], slot_all[:, :, :], float(SLOTS), float(OUTSIDE), ALU.is_lt, ALU.mult)\
                .then_inc(s["fits_done"], 1)
            dve.wait_ge(s["fits_done"], 1)
            dve.scalar_tensor_tensor(out=last_all[:, :], in0=fits[:, :, :].rearrange("p b k -> p (b k)"), scalar=-1.0,
                                     in1=expert_all[:, :, :].rearrange("p b k -> p (b k)"), op0=ALU.add, op1=ALU.add)\
                .then_inc(s["last_all_done"], 1)
            dve.wait_ge(s["slot_top_done"], 1)
            dve.tensor_scalar(overflow[:, :], slot_top[:, :], float(SLOTS), None, ALU.is_ge).then_inc(s["overflow_done"], 1)

            def picks_of_slots(e, q, n):
                dve.wait_ge(xg_in[q], 16 * (n + 1))
                if not isinstance(e, int) or e >= WB:
                    dve.wait_ge(row_out[q], 32 * n)
                dve.scalar_tensor_tensor(out=own[:, q], in0=xg[q][:, :, C:C + K], scalar=iota_e[:, bass.ds(e, 1)],
                                         in1=xg[q][:, :, C + K:RW], op0=ALU.is_equal, op1=ALU.mult)\
                    .then_inc(s["own_done"], 1)
                dve.wait_ge(s["own_done"], e + 1)
                dve.tensor_reduce(owned[:, q], own[:, q], AX.X, ALU.add).then_inc(s["owned_done"], 1)
                dve.wait_ge(s["owned_done"], e + 1)
                dve.tensor_scalar(pick_idx[:, q, :], owned[:, q], float(OUTSIDE), None, ALU.add)\
                    .then_inc(s["pick_ready"], 1)

            def gated(e, j):
                dve.wait_ge(s["f_s"], e + 1)
                dve.wait_ge(s["f_y"], e - 1) if not isinstance(e, int) or e >= 2 else None
                dve.tensor_tensor(act_t[:, j, :], sg[:, j, :], FG[j][:, 1, :], ALU.mult).then_inc(s["f_a"], 1)

            def rows_out_to_sbuf(e, q, n):
                dve.wait_ge(s["f_y"], e + 1)
                if not isinstance(e, int) or e >= WB:
                    dve.wait_ge(row_out[q], 32 * n)
                    dve.wait_ge(last_stored[q], 16 * n)
                dve.tensor_copy(yo[:, q, :, :], FY[q % 2]).then_inc(s["f_yo"], 1)

            for e in range(WB):
                picks_of_slots(e, e, 0)
                gated(e, e % 2)
                if e:
                    rows_out_to_sbuf(e - 1, e - 1, 0)
            with dve.Fori(1, E // WB - 1) as i:
                for q in range(WB):
                    picks_of_slots(WB * i + q, q, i)
                    gated(WB * i + q, q % 2)
                    rows_out_to_sbuf(WB * i + q - 1, (q - 1) % WB, i - (q == 0))
            for e in range(E - WB, E):
                picks_of_slots(e, e % WB, e // WB)
                gated(e, e % 2)
                rows_out_to_sbuf(e - 1, (e - 1) % WB, (e - 1) // WB)
            rows_out_to_sbuf(E - 1, WB - 1, E // WB - 1)

            dve.wait_ge(s["sh_b"], B // 2)
            dve.wait_ge(s["w_done"], B)

            for b in range(B):
                dve.wait_ge(gathered[b % GB], 16 * (b // GB + 1))
                dve.wait_ge(s["fixed"], b + 1)
                for k in range(K):
                    src = base_all[:, b, :] if k == 0 else part[:, b % 2, k - 1, :]
                    dst = res[:, b % 2, :] if k == K - 1 else part[:, b % 2, k, :]
                    if k:
                        dve.wait_ge(s["tail_part"], (K - 1) * b + k)
                    if k == K - 1 and b >= 2:
                        dve.wait_ge(out_done[b % 2], 16 * (b // 2))
                    dve.scalar_tensor_tensor(out=dst, in0=G[:, b % GB, k, :], scalar=w_all[:, b, k:k + 1], in1=src,
                                             op0=ALU.mult, op1=ALU.add)\
                        .then_inc(s["res_ready" if k == K - 1 else "tail_part"], 1)

        @block.tensor
        def _(pe):
            pe.wait_ge(s["ident_set"], 2)
            pe.wait_ge(s["col_in"], 48)
            nc.tensor.transpose(COLT, rows6[:, :], ident[0:3 * HC, 0:3 * HC]).then_inc(s["colT_ready"], 1)
            pe.wait_ge(s["gw_in"], 16)
            for h in range(HC):
                last = nc.tensor.transpose(GWT[:, h, :], gw[:, h * P:(h + 1) * P], ident[0:E, 0:E])
            last.then_inc(s["gwT_ready"], 1)
            pe.wait_ge(s["gwT_done"], 1)
            pe.wait_ge(s["tri_set"], 2)
            pe.wait_ge(s["consts"], 4)

            def to_channels(b, j):
                pe.wait_ge(s["ekv_ready"], b + 1)
                if b >= 2:
                    pe.wait_ge(s["nd_done"], 2 * b - 2)
                    pe.wait_ge(s["col0_done"], b - 1)
                for a, src in enumerate((ek, ekv)):
                    for h in range(HC):
                        last = nc.tensor.transpose(XT[j][:, a, h, :], src[:, j, h * P:(h + 1) * P], ident[:, :])
                last.then_inc(s["xt_ready"], 1)

            def to_tokens(b, j):
                pe.wait_ge(s["y_ready"], b + 1)
                if b >= 2:
                    pe.wait_ge(s["x1_ready"], b - 1)
                for h in range(HC):
                    last = nc.tensor.transpose(YT[j][:, h * P:(h + 1) * P], Y[:, j, h, :], ident[:, :])
                last.then_inc(s["yt_ready"], 1)

            def normed_to_channels(b, j):
                pe.wait_ge(s["n_ready"], b + 1)
                if b >= 2:
                    pe.wait_ge(s["hTall_done"], HC * (b - 1))
                for h in range(HC):
                    last = nc.tensor.transpose(NT[j][:, h, :], n_row[:, b % NR, h * P:(h + 1) * P], ident[:, :])
                last.then_inc(s["nt_ready"], 1)

            def logits(b, j):
                pe.wait_ge(s["hT_ready"], HC * (b + 1))
                if b >= 1:
                    pe.wait_ge(s["idx_done"], b)
                for h in range(HC):
                    last = nc.tensor.matmul(LG, hT[:, j, h, :], gwT[:, h, :], start=(h == 0), stop=(h == HC - 1))
                last.then_inc(s["lg_ready"], 1)

            def positions(b, j):
                pe.wait_ge(s["mask_ready"], b + 1)
                pe.wait_ge(s["before_ready"], b + 1)
                if b >= 1:
                    pe.wait_ge(s["over_done"], b)
                    pe.wait_ge(s["ga_done"], b)
                nc.tensor.matmul(PO, tri[:, :], mask[:, j, :], start=True, stop=False)
                nc.tensor.matmul(PO, ones[:, :], before[:, j, :], start=False, stop=True).then_inc(s["pos_ready"], 1)

            run([(-1, to_channels), (0, to_tokens), (1, normed_to_channels), (1, logits), (2, positions)])

            pe.wait_ge(s["sh_in"], 48)
            pe.wait_ge(s["hTall_done"], HC * B)
            pe.wait_ge(s["x1_ready"], B)
            for c in range(B // 2 + 1):
                if c < B // 2:
                    if c >= 2:
                        pe.wait_ge(s["sh_a"], c - 1)
                    for a in range(2):
                        for h in range(HC):
                            last = nc.tensor.matmul(FG[c % 2][:, a, :], sgu[:, h, a, :],
                                                    hT_all[:, h, 2 * c:2 * c + 2, :].rearrange("p b t -> p (b t)"),
                                                    start=(h == 0), stop=(h == HC - 1))
                    last.then_inc(s["sh_g"], 1)
                if c >= 1:
                    d = c - 1
                    pe.wait_ge(s["sh_a"], d + 1)
                    if d >= 2:
                        pe.wait_ge(s["sh_b"], d - 1)
                    for a in range(2):
                        last = nc.tensor.matmul(FY[d % 2][:, a, :], act_t[:, d % 2, a * P:(a + 1) * P], sdn[:, :],
                                                start=True, stop=True)
                    last.then_inc(s["sh_y"], 1)
            pe.wait_ge(s["sh_b"], B // 2)
            pe.wait_ge(s["nd_done"], 2 * B)

            def rows_to_channels(e, q, n):
                pe.wait_ge(xg_in[q], 16 * (n + 1))
                if not isinstance(e, int) or e >= 2:
                    pe.wait_ge(s["f_x"], 2 * e - 2)
                for h in range(HC):
                    for a in range(2):
                        last = nc.tensor.transpose(FX[q % 2][:, h, a * P:(a + 1) * P], xg[q][:, a, h * P:(h + 1) * P],
                                                   ident[:, :])
                last.then_inc(s["f_xt"], 1)

            def gate_up(e, q, n):
                pe.wait_ge(w_in[q], 32 * (n + 1))
                pe.wait_ge(s["f_x"], 2 * e + 2)
                if not isinstance(e, int) or e >= 2:
                    pe.wait_ge(s["f_a"], e - 1)
                for a in range(2):
                    for h in range(HC):
                        last = nc.tensor.matmul(FG[q % 2][:, a, :], w13b[q][:, h, a, :], xT[:, q % 2, h, :],
                                                start=(h == 0), stop=(h == HC - 1))
                last.then_inc(s["f_g"], 1)

            def down(e, q):
                pe.wait_ge(s["f_a"], e + 1)
                if not isinstance(e, int) or e >= 2:
                    pe.wait_ge(s["f_yo"], e - 1)
                for a in range(2):
                    last = nc.tensor.matmul(FY[q % 2][:, a, :], act_t[:, q % 2, a * P:(a + 1) * P], w2b[q][:, :],
                                            start=True, stop=True)
                last.then_inc(s["f_y"], 1)

            rows_to_channels(0, 0, 0)
            for e in range(WB):
                rows_to_channels(e + 1, (e + 1) % WB, (e + 1) // WB)
                gate_up(e, e, 0)
                if e:
                    down(e - 1, e - 1)
            with pe.Fori(1, E // WB - 1) as i:
                for q in range(WB):
                    rows_to_channels(WB * i + q + 1, (q + 1) % WB, i + (q == WB - 1))
                    gate_up(WB * i + q, q, i)
                    down(WB * i + q - 1, (q - 1) % WB)
            for e in range(E - WB, E):
                if e < E - 1:
                    rows_to_channels(e + 1, (e + 1) % WB, (e + 1) // WB)
                gate_up(e, e % WB, e // WB)
                down(e - 1, (e - 1) % WB)
            down(E - 1, WB - 1)


_INS = ['x', 'ctx_2048', 'L0_xattn_time_decay', 'L0_xattn_time_first', 'L0_ffn_norm_w', 'L0_ffn_gate_w',
        'L0_ffn_w13', 'L0_ffn_w2', 'L0_ffn_shared_gate_w', 'L0_ffn_shared_up_w', 'L0_ffn_shared_down_w']


def kernel(**inputs):
    import numpy as _np
    import concourse.bacc as _bacc
    from concourse import mybir as _mybir
    from concourse.bass_utils import run_bass_kernel_spmd as _run

    nc = _bacc.Bacc("TRN2", target_bir_lowering=False, num_devices=1)
    arrays, args = {}, []
    for name in _INS:
        a = _np.ascontiguousarray(inputs[name])
        arrays[f"in_{name}_dram"] = a
        args.append(nc.dram_tensor(f"in_{name}_dram", a.shape, _mybir.dt.from_np(a.dtype), kind="ExternalInput").ap())
    args.append(nc.dram_tensor("out_dram", (B, T, C), _mybir.dt.float32, kind="ExternalOutput").ap())
    xattn_moe(nc, *args)
    r = _run(nc, [arrays], core_ids=[0])
    return r.results[0]["out_dram"]
```

```python
import concourse.bass as bass
from concourse import mybir
from contextlib import ExitStack

F32 = mybir.dt.float32
BF16 = mybir.dt.bfloat16
I32 = mybir.dt.int32
U32 = mybir.dt.uint32
ALU = mybir.AluOpType
ACT = mybir.ActivationFunctionType
AX = mybir.AxisListType

P = 128
B, T, C = 8, 128, 256
E, K, F = 32, 4, 128
CAP = 2 * B * T * K // E
HC = C // P
ROWS_E = B * T
LN_EPS, RMS_EPS = 1e-5, 1e-6
EXP_LN = 6
PICKS = B * T * K
RW = C + 2 * K
OUTSIDE = 16384
U_MAX = 60.0
POOL_SUMS = (1, 3, 6)
FIRST = 2
W2L = 4
SHARED_AFTER = 5
WB = 4


def xattn_moe(nc, x, ctx_in, time_decay, time_first, norm_w, gate_w, w13, w2, sh_gate, sh_up, sh_down, out):
    ctx = ExitStack()
    with ctx:
        def sb(name, shape, dt=F32):
            return ctx.enter_context(nc.sbuf_tensor(name, shape, dt))

        def sem(name):
            return ctx.enter_context(nc.semaphore(name))

        rows_in = nc.dram_tensor("rows_in", (E * ROWS_E, RW), F32, kind="Internal").ap()
        rows_out = nc.dram_tensor("rows_out", (PICKS, C), F32, kind="Internal").ap()
        last_rows = nc.dram_tensor("last_rows", (E, C), F32, kind="Internal").ap()

        x_all = sb("x_all", [P, B, C])
        v_all = sb("v_all", [P, B, C])
        base_all = sb("base_all", [P, B, C])
        gu_all = sb("gu_all", [P, 2, B, T])
        w_all = sb("w_all", [P, B, K])
        slot_all = sb("slot_all", [P, B, K], I32)
        tags = sb("tags", [P, B, 2 * K])
        beyond = sb("beyond", [P, B, K])
        fits = sb("fits", [P, B, K])
        last_all = sb("last_all", [P, B * K], I32)
        late_all = sb("late_all", [P, B * K], I32)
        big = sb("big", [P, E], I32)
        slot_max = sb("slot_max", [P, 1])
        slot_top = sb("slot_top", [P, 1])
        overflow = sb("overflow", [P, 1], I32)

        ident = sb("ident", [P, P])
        tri = sb("tri", [P, P], BF16)
        ones = sb("ones", [P, P], BF16)
        iota_e = sb("iota_e", [P, E])
        slot0 = sb("slot0", [P, E])
        rows6 = sb("rows6", [3 * HC, P])
        cols6 = sb("cols6", [P, 3 * HC])
        td, tf, nw = (cols6[:, HC * m:HC * (m + 1)] for m in range(3))
        etd = sb("etd", [P, HC])
        dcol = sb("dcol", [P, HC])
        ucol = sb("ucol", [P, HC])
        tfc = sb("tfc", [P, HC])
        low = sb("low", [P, HC])
        inv_top = sb("inv_top", [P, HC])
        top = sb("top", [P, HC])
        decay = sb("decay", [P, 2, HC, T])
        gw = sb("gw", [E, C])
        gwT = sb("gwT", [P, HC, E])
        sgu = sb("sgu", [P, HC, 2, F])
        sdn = sb("sdn", [P, C])
        zeros = sb("zeros", [P, 4 * RW])
        neg_half = sb("neg_half", [P, B])

        st1 = sb("st1", [P, B, 6])
        mv1 = sb("mv1", [P, B, 2])
        ve1 = sb("ve1", [P, B])
        rstd1 = sb("rstd1", [P, B])
        nb1 = sb("nb1", [P, B])

        ek = sb("ek", [P, 2, C])
        ekv = sb("ekv", [P, 2, C])
        S = sb("S", [P, 2, 2, HC, T])
        ND = sb("ND", [P, 2, 2, HC, T])
        ln_den = sb("ln_den", [P, 2, HC, T])
        R0 = sb("R0", [P, 2, HC, T])
        DR = sb("DR", [P, 2, HC, T])
        R = sb("R", [P, 2, HC, T])
        Y = sb("Y", [P, 2, HC, T])
        x1 = sb("x1", [P, 2, C])
        st2 = sb("st2", [P, 2, 6])
        mv2 = sb("mv2", [P, 2, 2])
        ve2 = sb("ve2", [P, 2, 2])
        var_mul = sb("var_mul", [P, 2])
        var_add = sb("var_add", [P, 2])
        rs2 = sb("rs2", [P, 2, 2])
        one_rs2 = sb("one_rs2", [P, 2, 1])
        nm2 = sb("nm2", [P, 2, 1])
        nb2 = sb("nb2", [P, 2, 2])
        n_row = sb("n_row", [P, B, RW])
        hT = sb("hT", [P, 2, HC, T])
        top8 = sb("top8", [P, 2, 8])
        idx8 = sb("idx8", [P, 2, 8], U32)
        nmax = sb("nmax", [P, 2, 1])
        ew = sb("ew", [P, B, K])
        esum = sb("esum", [P, B])
        rsum = sb("rsum", [P, B])
        onehot = sb("onehot", [P, 2, K, E])
        mask = sb("mask", [P, B, E], BF16)
        slots = sb("slots", [P, 2, E])
        picked = sb("picked", [P, 2, K, E])
        last_idx = sb("last_idx", [P, 2], I32)
        late_row = sb("late_row", [P, C])

        w13b = [sb(f"w13b{q}", [P, HC, 2, F]) for q in range(WB)]
        w2_all = sb("w2_all", [P, E, C])
        xg = [sb(f"xg{q}", [P, 2, RW]) for q in range(WB)]
        own = sb("own", [P, WB, 2, K])
        owned = sb("owned", [P, WB, 2])
        pick_idx = sb("pick_idx", [P, WB, 2], I32)
        xT = sb("xT", [P, 2, HC, CAP])
        sg = sb("sg", [P, 2, CAP])
        act_t = sb("act_t", [P, 2, CAP])
        sg_all = sb("sg_all", [P, B, T])
        yo = sb("yo", [P, WB, 2, C])
        G = sb("G", [P, B, K, C])
        res = sb("res", [P, B, C])
        part = sb("part", [P, 2, K - 1, C])
        pool_part = sb("pool_part", [P, K - 1, C])

        bank = [ctx.enter_context(nc.psum_tensor(f"bank{i}", [P, 512], F32)) for i in range(8)]
        XT = [bank[j][:, :].rearrange("p (a h t) -> p a h t", a=2, h=HC) for j in range(2)]
        YT = [bank[2 + j][:, 0:C] for j in range(2)]
        NT = [bank[4 + j][:, 0:C].rearrange("p (h t) -> p h t", h=HC) for j in range(2)]
        LG = bank[6][:, 0:E]
        PO = bank[6][:, 64:64 + E]
        TOT = bank[6][:, 128:128 + E]
        SGU = bank[7][:, 0:2 * T].rearrange("p (a t) -> p a t", a=2)
        GWT = bank[7][:, 320:320 + HC * E].rearrange("p (h e) -> p h e", h=HC)
        COLT = bank[7][:, 256:256 + 3 * HC]
        FX = [bank[j][:, :].rearrange("p (h s) -> p h s", h=HC) for j in range(2)]
        FG = [bank[2 + j][:, :].rearrange("p (a s) -> p a s", a=2) for j in range(2)]
        FY = [bank[4 + j][:, :].rearrange("p (a c) -> p a c", a=2) for j in range(2)]

        names = """
            held_pool colT_ready cols6_done x0_in x1_in v0_in v1_in col_in gw_in sh_in sdn_in zero_set consts
            ident_set tri_set st1_done mv1_done low_done ve1_done rstd1_done nb1_done decay_e tf_clamped cols_done
            decay_done gwT_ready gwT_done ek_ready ekv_ready xt_ready col0_done scan_done nd_done ln_ready r0_ready
            dr_done recip_done y_ready yt_ready x1_ready st2_done mv2_done ve2_done rs2_done nm2_done one_rs2_done
            nb2_done n_ready base_ready nt_ready hT_ready lg_ready top_ready idx_done expert_ready nmax_done
            ew_ready rsum_done w_done tagged onehot_done mask_ready pos_ready slots_done picked_done slot_ready
            own_done owned_done pick_ready fits_done last_all_done last_set slot_max_done slot_top_done
            overflow_done fixed pickno_ready gu_ready gu_done sh_s sh_a tot_ready big_done beyond_done sh_y sh_b
            f_xt f_x f_g f_s f_a f_y f_yo tail_part res_ready weighted pool_part_done pool_res_ready""".split()
        s = {n: sem(n) for n in names}
        scattered = [sem(f"scattered{b}") for b in range(B)]
        w_in = [sem(f"w_in{q}") for q in range(WB)]
        w2_in = [sem(f"w2_in{g}") for g in range(W2L)]
        xg_in = [sem(f"xg_in{q}") for q in range(WB)]
        row_out = [sem(f"row_out{q}") for q in range(WB)]
        gathered = [sem(f"gathered{b}") for b in range(B + 1)]
        last_stored = [sem(f"last_stored{q}") for q in range(WB)]
        zeroed = [sem(f"zeroed{a}") for a in range(2)]
        last_in = sem("last_in")
        late_out = sem("late_out")
        out_done = sem("out_done")
        pool_out_done = sem("pool_out_done")

        def run(stages):
            for n in range(min(lag for lag, _ in stages), B + max(lag for lag, _ in stages)):
                for lag, stage in stages:
                    if 0 <= n - lag < B:
                        stage(n - lag, (n - lag) % 2)

        def later(e, n):
            return not isinstance(e, int) or e >= n

        block = ctx.enter_context(nc.Block())

        @block.sync
        def _(sp):
            xv = x.rearrange("b t c -> t b c")
            vv = ctx_in.rearrange("b t c -> t b c")
            for lo, hi, x_in, v_in in ((0, FIRST, "x0_in", "v0_in"), (FIRST, B, "x1_in", "v1_in")):
                sp.dma_start(x_all[:, lo:hi, :], xv[:, lo:hi, :]).then_inc(s[x_in], 16)
                if lo == 0:
                    sp.dma_start(gw[:, :], gate_w).then_inc(s["gw_in"], 16)
                sp.dma_start(v_all[:, lo:hi, :], vv[:, lo:hi, :]).then_inc(s[v_in], 16)
            sp.dma_start(sgu[:, :, 0, :], sh_gate.rearrange("(h p) f -> p h f", p=P)).then_inc(s["sh_in"], 16)
            sp.dma_start(sgu[:, :, 1, :], sh_up.rearrange("(h p) f -> p h f", p=P)).then_inc(s["sh_in"], 16)
            sp.wait_ge(s["zero_set"], 1)
            zv = rows_in.rearrange("(e n) c -> n e c", n=ROWS_E)
            for a in range(2):
                for e in range(0, E, 2):
                    sp.dma_start(zv[a * P:(a + 1) * P, e:e + 2, :],
                                 zeros[:, 0:2 * RW].rearrange("p (e c) -> p e c", e=2)).then_inc(zeroed[a], 16)

            sp.dma_start(sdn[:, :], sh_down).then_inc(s["sdn_in"], 16)

            def load_weights(e, q):
                sp.dma_start(w13b[q][:, :, :, :].rearrange("p h a f -> p h (a f)"),
                             w13[bass.ds(e, 1)].rearrange("o (h p) f -> p (o h) f", p=P)).then_inc(w_in[q], 16)

            def load_rows(e, q):
                sp.dma_start(xg[q][:, :, :],
                             rows_in[bass.ds(e * ROWS_E, CAP), :].rearrange("(a p) c -> p a c", p=P))\
                    .then_inc(xg_in[q], 16)

            def store_last(e, q):
                sp.wait_ge(s["f_yo"], e + 1)
                sp.dma_start(last_rows[bass.ds(e, 1), :], yo[P - 1:P, q, 1, :]).then_inc(last_stored[q], 16)

            for q in range(WB):
                load_weights(q, q)
            n = E // W2L
            for g in range(W2L):
                sp.dma_start(w2_all[:, g * n:(g + 1) * n, :], w2[g * n:(g + 1) * n].rearrange("e p c -> p e c"))\
                    .then_inc(w2_in[g], 16)
            for b in range(B):
                sp.wait_ge(scattered[b], 16 * K)
            for q in range(WB):
                load_rows(q, q)

            def refill(e, q, n, first=False):
                sp.wait_ge(s["f_xt"], e + 1)
                sp.wait_ge(s["own_done"], e + 1)
                load_rows(e + WB, q)
                if not first:
                    sp.wait_ge(s["f_g"], e)
                    load_weights(e - 1 + WB, (q - 1) % WB)
                    store_last(e - 1, (q - 1) % WB)

            for q in range(WB):
                refill(q, q, 0, q == 0)
            with sp.Fori(1, E // WB - 1) as i:
                for q in range(WB):
                    refill(WB * i + q, q, i)
            sp.wait_ge(s["f_g"], E - WB)
            load_weights(E - 1, WB - 1)
            for e in range(E - WB - 1, E):
                store_last(e, e % WB)
            ov = out.rearrange("b t c -> t b c")
            for q in range(WB):
                sp.wait_ge(row_out[q], 32 * E // WB)

            sp.wait_ge(s["fixed"], 1)

            picks = rows_out.rearrange("(b p k) c -> b p k c", b=B, k=K)
            for b in range(B):
                for n, ks in enumerate((slice(0, K),) if b < B - 1 else (slice(0, K // 2), slice(K // 2, K))):
                    sp.dma_start(G[:, b, ks], picks[b, :, ks, :]).then_inc(gathered[b + n], 16)
            mine = [b for b in range(B) if b not in POOL_SUMS]
            for n, b in enumerate(mine):
                sp.wait_ge(s["res_ready"], n + 1)
                sp.dma_start(ov[:, b:b + 1, :], res[:, b:b + 1, :]).then_inc(out_done, 16)
            sp.wait_ge(out_done, 16 * len(mine))
            for q in range(WB):
                sp.wait_ge(last_stored[q], 16 * E // WB)

        @block.gpsimd
        def _(pool):
            pool.memset(zeros[:, :], 0.0).then_inc(s["zero_set"], 1)
            pool.memset(ident[:, :], 0.0).then_inc(s["ident_set"], 1)
            pool.memset(tri[:, :], 1.0).then_inc(s["tri_set"], 1)
            pool.memset(ones[:, :], 1.0).then_inc(s["consts"], 1)
            pool.memset(late_row[:, :], 0.0).then_inc(s["consts"], 1)
            pool.memset(neg_half[:, :], -0.5).then_inc(s["consts"], 1)
            for m, (mul, add) in enumerate(((1.0, LN_EPS), (1.0 + RMS_EPS, LN_EPS * RMS_EPS))):
                pool.memset(var_mul[:, m:m + 1], mul).then_inc(s["consts"], 1)
                pool.memset(var_add[:, m:m + 1], add).then_inc(s["consts"], 1)
            pool.iota(iota_e[:, :], [[1, E]], base=1, channel_multiplier=0,
                      allow_small_or_imprecise_dtypes=True).then_inc(s["consts"], 1)
            pool.iota(slot0[:, :], [[ROWS_E, E]], base=0, channel_multiplier=0,
                      allow_small_or_imprecise_dtypes=True).then_inc(s["consts"], 1)
            pool.iota(tags[:, :, K:2 * K], [[T * K, B], [1, K]], base=-OUTSIDE, channel_multiplier=K,
                      allow_small_or_imprecise_dtypes=True).then_inc(s["pickno_ready"], 1)
            pool.wait_ge(s["ident_set"], 1)
            pool.affine_select(out=ident[:, :], in_=ident[:, :], compare_op=ALU.not_equal, fill=1.0, base=0,
                               pattern=[[-1, P]], channel_multiplier=1).then_inc(s["ident_set"], 1)
            pool.wait_ge(s["tri_set"], 1)
            pool.affine_select(out=tri[:, :], in_=tri[:, :], compare_op=ALU.is_gt, fill=0.0, base=0,
                               pattern=[[1, P]], channel_multiplier=-1).then_inc(s["tri_set"], 1)
            pool.wait_ge(s["consts"], 9)
            for n, (lo, hi) in enumerate(((0, FIRST), (FIRST, B))):
                pool.wait_ge(s["mv1_done"], hi)
                pool.tensor_scalar(ve1[:, lo:hi], mv1[:, lo:hi, 1], LN_EPS, 1.0, ALU.add, ALU.mult)\
                    .then_inc(s["ve1_done"], 1)
                pool.wait_ge(s["ve1_done"], n + 1)
                pool.tensor_tensor(rstd1[:, lo:hi], ve1[:, lo:hi], neg_half[:, lo:hi], ALU.pow)\
                    .then_inc(s["rstd1_done"], 1)

            def norm_scales(b, j):
                pool.wait_ge(s["ve2_done"], b + 1)
                pool.tensor_tensor(rs2[:, j, :], ve2[:, j, :], neg_half[:, 0:2], ALU.pow).then_inc(s["rs2_done"], 1)

            def scatter(b, j):
                pool.wait_ge(zeroed[0], 16 * E // 2)
                if b:
                    pool.wait_ge(zeroed[1], 16 * E // 2)
                pool.wait_ge(s["n_ready"], b + 1)
                pool.wait_ge(s["tagged"], b + 1)
                pool.wait_ge(s["slot_ready"], b + 1)
                for k in range(K):
                    pool.indirect_dma_start(rows_in, bass.IndirectOffsetOnAxis(ap=slot_all[:, b, k:k + 1], axis=0),
                                            n_row[:, b, :], None)\
                        .then_inc(scattered[b], 16)

            run([(2, norm_scales), (4, scatter)])

            pool.wait_ge(s["slot_max_done"], 1)
            pool.partition_all_reduce(slot_top[:, :], slot_max[:, :], P, bass.bass_isa.ReduceOp.max)\
                .then_inc(s["slot_top_done"], 1)

            def scatter_out(e, q):
                pool.wait_ge(s["pick_ready"], e + 1)
                pool.wait_ge(s["f_yo"], e + 1)
                pool.sem_inc(s["held_pool"], 1)
                for a in range(2):
                    pool.indirect_dma_start(rows_out, bass.IndirectOffsetOnAxis(ap=pick_idx[:, q, a:a + 1], axis=0),
                                            yo[:, q, a, :], None, bounds_check=PICKS - 1, oob_is_err=False)\
                        .then_inc(row_out[q], 16)

            pool.wait_ge(s["overflow_done"], 1)
            pool.wait_ge(s["last_all_done"], 2)
            flag = pool.value_load(overflow[0:1, 0:1], min_val=0, max_val=1)

            with pool.Fori(0, E // WB) as i:
                for q in range(WB):
                    scatter_out(WB * i + q, q)

            with pool.If(flag != 0):
                for q in range(WB):
                    pool.wait_ge(last_stored[q], 16 * E // WB)
                for m in range(B * K):
                    pool.tensor_copy(last_idx[:, 0:1], last_all[:, m:m + 1]).then_inc(s["last_set"], 1)
                    pool.tensor_copy(last_idx[:, 1:2], late_all[:, m:m + 1]).then_inc(s["last_set"], 1)
                    pool.wait_ge(s["last_set"], 2 * m + 2)
                    pool.indirect_dma_start(late_row[:, :], None, last_rows,
                                            bass.IndirectOffsetOnAxis(ap=last_idx[:, 0:1], axis=0),
                                            bounds_check=E - 1, oob_is_err=False).then_inc(last_in, 16)
                    pool.wait_ge(last_in, 16 * (m + 1))
                    pool.indirect_dma_start(rows_out, bass.IndirectOffsetOnAxis(ap=last_idx[:, 1:2], axis=0),
                                            late_row[:, :], None, bounds_check=PICKS - 1, oob_is_err=False)\
                        .then_inc(late_out, 16)
                    pool.wait_ge(late_out, 16 * (m + 1))
            pool.sem_inc(s["fixed"], 1)

            for n, b in enumerate(POOL_SUMS):
                for k in range(K):
                    src = base_all[:, b, :] if k == 0 else pool_part[:, k - 1, :]
                    dst = res[:, b, :] if k == K - 1 else pool_part[:, k, :]
                    pool.wait_ge(s["weighted"], K * n + k + 1)
                    if k:
                        pool.wait_ge(s["pool_part_done"], (K - 1) * n + k)
                    pool.tensor_tensor(dst, G[:, b, k, :], src, ALU.add)\
                        .then_inc(s["pool_res_ready" if k == K - 1 else "pool_part_done"], 1)

        @block.scalar
        def _(act):
            for m, vec in enumerate((time_decay, time_first, norm_w)):
                act.dma_start(rows6[HC * m:HC * (m + 1), :], vec.rearrange("(h p) -> h p", p=P)).then_inc(s["col_in"], 16)
            act.add_instruction(mybir.InstLoadActFuncSet(name=nc.get_next_instruction_name(), act_func_set_id=EXP_LN))
            act.wait_ge(s["colT_ready"], 1)
            act.activation(cols6[:, :], COLT, ACT.Copy).then_inc(s["cols6_done"], 1)
            act.wait_ge(s["cols6_done"], 1)
            act.activation(etd[:, :], td, ACT.Exp).then_inc(s["decay_e"], 1)
            act.wait_ge(s["decay_e"], 1)
            act.activation(dcol[:, :], etd[:, :], ACT.Exp, scale=-1.0).then_inc(s["cols_done"], 1)
            act.wait_ge(s["tf_clamped"], 1)
            act.activation(ucol[:, :], tfc[:, :], ACT.Exp).then_inc(s["cols_done"], 1)
            act.wait_ge(s["low_done"], 1)
            act.activation(top[:, :], low[:, :], ACT.Exp, scale=-1.0).then_inc(s["cols_done"], 1)
            act.activation(inv_top[:, :], low[:, :], ACT.Exp).then_inc(s["cols_done"], 1)
            act.wait_ge(s["gwT_ready"], 1)
            act.activation(gwT[:, :, :], GWT, ACT.Copy).then_inc(s["gwT_done"], 1)
            act.wait_ge(s["cols_done"], 4)
            act.wait_ge(s["pickno_ready"], 1)

            def exp_k(b, j):
                act.wait_ge(s["nb1_done"], 1 if b < FIRST else 2)
                if b >= 2:
                    act.wait_ge(s["xt_ready"], b - 1)
                act.activation(ek[:, j, :], x_all[:, bass.ds(b, 1), :].rearrange("p o c -> p (o c)"), ACT.Exp,
                               bias=nb1[:, bass.ds(b, 1)], scale=rstd1[:, bass.ds(b, 1)]).then_inc(s["ek_ready"], 1)

            def first_reciprocal(b, j):
                act.wait_ge(s["nd_done"], HC * (b + 1))
                act.wait_ge(s["col0_done"], b + 1)
                if b >= 2:
                    act.wait_ge(s["y_ready"], b - 1)
                    act.wait_ge(s["r0_ready"], HC * (b - 1))
                for h in range(HC):
                    act.activation(ln_den[:, j, h, :], ND[:, j, 0, h, :], ACT.Ln, scale=inv_top[:, h:h + 1])\
                        .then_inc(s["ln_ready"], 1)
                for h in range(HC):
                    act.wait_ge(s["ln_ready"], HC * b + h + 1)
                    act.activation(R0[:, j, h, :], ln_den[:, j, h, :], ACT.Exp, bias=low[:, h:h + 1], scale=-1.0)\
                        .then_inc(s["r0_ready"], 1)

            def shifts(b, j):
                act.wait_ge(s["mv2_done"], b + 1)
                if b >= 2:
                    act.wait_ge(s["base_ready"], b - 1)
                act.activation(nm2[:, j, :], mv2[:, j, 0:1], ACT.Copy, scale=-1.0).then_inc(s["nm2_done"], 1)
                act.wait_ge(s["rs2_done"], b + 1)
                act.activation(one_rs2[:, j, :], rs2[:, j, 0:1], ACT.Copy, bias=1.0).then_inc(s["one_rs2_done"], 1)
                act.wait_ge(s["nm2_done"], b + 1)
                act.activation(nb2[:, j, :], rs2[:, j, :], ACT.Copy, scale=nm2[:, j, :]).then_inc(s["nb2_done"], 1)

            def normed(b, j):
                act.wait_ge(s["nb2_done"], b + 1)
                act.activation(n_row[:, b, 0:C], x1[:, j, :], ACT.Identity, bias=nb2[:, j, 1:2],
                               scale=rs2[:, j, 1:2]).then_inc(s["n_ready"], 1)

            def base(b, j):
                act.wait_ge(s["one_rs2_done"], b + 1)
                act.activation(base_all[:, bass.ds(b, 1), :].rearrange("p o c -> p (o c)"), x1[:, j, :], ACT.Identity,
                               bias=nb2[:, j, 0:1], scale=one_rs2[:, j, :]).then_inc(s["base_ready"], 1)

            def normed_T(b, j):
                act.wait_ge(s["nt_ready"], b + 1)
                if b >= 2:
                    act.wait_ge(s["gu_ready"], b - 1)
                for h in range(HC):
                    act.activation(hT[:, j, h, :], NT[j][:, h, :], ACT.Copy, scale=nw[:, h:h + 1])\
                        .then_inc(s["hT_ready"], 1)

            def negative_max(b, j):
                act.wait_ge(s["top_ready"], b + 1)
                if b >= 2:
                    act.wait_ge(s["ew_ready"], b - 1)
                act.activation(nmax[:, j, :], top8[:, j, 0:1], ACT.Copy, scale=-1.0).then_inc(s["nmax_done"], 1)

            def pick_weights(b, j):
                act.wait_ge(s["nmax_done"], b + 1)
                act.activation(ew[:, b, :], top8[:, j, 0:K], ACT.Exp, bias=nmax[:, j, :],
                               accum_out=esum[:, b:b + 1]).then_inc(s["ew_ready"], 1)

            def tag_rows(b, j):
                act.wait_ge(s["expert_ready"], b + 1)
                act.activation(n_row[:, b, C:RW], tags[:, b, :], ACT.Copy).then_inc(s["tagged"], 1)

            def shared_to_sbuf(b, j):
                act.wait_ge(s["gu_ready"], b + 1)
                act.activation(gu_all[:, :, b, :], SGU, ACT.Copy).then_inc(s["gu_done"], 1)

            run([(-2, exp_k), (3, negative_max), (2, shifts), (2, normed), (3, pick_weights), (0, first_reciprocal),
                 (2, normed_T), (3, shared_to_sbuf), (3, tag_rows), (2, base)])

            act.wait_ge(s["gu_done"], B)
            act.activation(sg_all[:, :, :], gu_all[:, 0], ACT.Silu).then_inc(s["sh_s"], 1)

            def rows_to_sbuf(e, j):
                act.wait_ge(s["f_xt"], e + 1)
                if later(e, 2):
                    act.wait_ge(s["f_g"], e - 1)
                for h in range(HC):
                    act.activation(xT[:, j, h, :], FX[j][:, h, :], ACT.Copy, scale=nw[:, h:h + 1]).then_inc(s["f_x"], 1)

            def silu(e, j):
                act.wait_ge(s["f_g"], e + 1)
                if later(e, 2):
                    act.wait_ge(s["f_a"], e - 1)
                act.activation(sg[:, j, :], FG[j][:, 0, :], ACT.Silu).then_inc(s["f_s"], 1)

            rows_to_sbuf(0, 0)
            for e in range(WB):
                rows_to_sbuf(e + 1, (e + 1) % 2)
                silu(e, e % 2)
            with act.Fori(1, E // WB - 1) as i:
                for q in range(WB):
                    rows_to_sbuf(WB * i + q + 1, (q + 1) % 2)
                    silu(WB * i + q, q % 2)
            for e in range(E - WB, E):
                if e < E - 1:
                    rows_to_sbuf(e + 1, (e + 1) % 2)
                silu(e, e % 2)

            act.wait_ge(s["sh_b"], B // 2)
            act.wait_ge(s["w_done"], 1)
            for b in POOL_SUMS:
                act.wait_ge(gathered[b], 16)
                for k in range(K):
                    act.activation(G[:, b, k, :], G[:, b, k, :], ACT.Copy, scale=w_all[:, b, k:k + 1])\
                        .then_inc(s["weighted"], 1)
            ov = out.rearrange("b t c -> t b c")
            for n, b in enumerate(POOL_SUMS):
                act.wait_ge(s["pool_res_ready"], n + 1)
                act.dma_start(ov[:, b:b + 1, :], res[:, b:b + 1, :]).then_inc(pool_out_done, 16)
            act.wait_ge(pool_out_done, 16 * len(POOL_SUMS))

        @block.vector
        def _(dve):
            def first_shift(n, lo, hi):
                dve.wait_ge(s["mv1_done"], hi)
                dve.wait_ge(s["rstd1_done"], n + 1)
                dve.scalar_tensor_tensor(out=nb1[:, lo:hi], in0=mv1[:, lo:hi, 0], scalar=-1.0, in1=rstd1[:, lo:hi],
                                         op0=ALU.mult, op1=ALU.mult).then_inc(s["nb1_done"], 1)

            def first_stats(lo, hi):
                for b in range(lo, hi):
                    dve.bn_stats(st1[:, b, :], x_all[:, b, :]).then_inc(s["st1_done"], 1)
                dve.wait_ge(s["st1_done"], hi)
                for b in range(lo, hi):
                    dve.bn_aggr(mv1[:, b, :], st1[:, b, :]).then_inc(s["mv1_done"], 1)

            dve.wait_ge(s["x0_in"], 16)
            first_stats(0, FIRST)
            dve.wait_ge(s["cols6_done"], 1)
            dve.tensor_scalar(tfc[:, :], tf, U_MAX, -U_MAX, ALU.min, ALU.max).then_inc(s["tf_clamped"], 1)
            dve.wait_ge(s["tf_clamped"], 1)
            dve.tensor_scalar(low[:, :], tfc[:, :], 0.0, -1.0, ALU.max, ALU.mult).then_inc(s["low_done"], 1)
            first_shift(0, 0, FIRST)
            dve.wait_ge(s["cols_done"], 1)
            for h in range(HC):
                dve.tensor_copy(decay[:, :, h, 1:T], dcol[:, h:h + 1].rearrange("p (a b) -> p a b", a=1)
                                .to_broadcast([P, 2, T - 1])).then_inc(s["decay_done"], 1)
            dve.memset(decay[:, :, :, 0:1], 0.0).then_inc(s["decay_done"], 1)
            dve.wait_ge(s["decay_done"], HC + 1)
            dve.wait_ge(s["cols_done"], 4)
            dve.wait_ge(s["consts"], 9)

            def others_stats(b, j):
                if b == 0:
                    dve.wait_ge(s["x1_in"], 16)
                    first_stats(FIRST, B)

            def others_shift(b, j):
                if b == 0:
                    first_shift(1, FIRST, B)

            def times_v(b, j):
                if b in (0, FIRST):
                    dve.wait_ge(s["v1_in" if b else "v0_in"], 16)
                dve.wait_ge(s["ek_ready"], b + 1)
                dve.tensor_tensor(ekv[:, j, :], ek[:, j, :], v_all[:, b, :], ALU.mult).then_inc(s["ekv_ready"], 1)

            def scan(b, j):
                dve.wait_ge(s["xt_ready"], b + 1)
                if b >= 2:
                    dve.wait_ge(s["nd_done"], HC * (b - 1))
                dve.tensor_tensor_scan(S[:, j].rearrange("p a h t -> p (a h t)"),
                                       decay[:, :, :, :].rearrange("p a h t -> p (a h t)"),
                                       XT[j].rearrange("p a h t -> p (a h t)"), 0.0, ALU.mult, ALU.add)\
                    .then_inc(s["scan_done"], 1)

            def num_den(b, j):
                if b >= 2:
                    dve.wait_ge(s["y_ready"], b - 1)
                dve.tensor_tensor(ND[:, j, :, :, 0], XT[j][:, :, :, 0], top[:, :].unsqueeze(1).to_broadcast([P, 2, HC]),
                                  ALU.mult).then_inc(s["col0_done"], 1)
                dve.wait_ge(s["scan_done"], b + 1)
                for h in range(HC):
                    dve.scalar_tensor_tensor(out=ND[:, j, :, h, 1:T], in0=XT[j][:, :, h, 1:T], scalar=ucol[:, h:h + 1],
                                             in1=S[:, j, :, h, 0:T - 1], op0=ALU.mult, op1=ALU.add)\
                        .then_inc(s["nd_done"], 1)

            def newton_product(b, j):
                dve.wait_ge(s["r0_ready"], HC * (b + 1))
                dve.wait_ge(s["nd_done"], HC * (b + 1))
                if b >= 2:
                    dve.wait_ge(s["recip_done"], b - 1)
                dve.scalar_tensor_tensor(out=DR[:, j], in0=ND[:, j, 0], scalar=-1.0, in1=R0[:, j],
                                         op0=ALU.mult, op1=ALU.mult).then_inc(s["dr_done"], 1)

            def newton_step(b, j):
                dve.wait_ge(s["dr_done"], b + 1)
                if b >= 2:
                    dve.wait_ge(s["y_ready"], b - 1)
                dve.scalar_tensor_tensor(out=R[:, j], in0=DR[:, j], scalar=2.0, in1=R0[:, j],
                                         op0=ALU.add, op1=ALU.mult).then_inc(s["recip_done"], 1)

            def quotient(b, j):
                dve.wait_ge(s["recip_done"], b + 1)
                if b >= 2:
                    dve.wait_ge(s["yt_ready"], b - 1)
                dve.tensor_tensor(Y[:, j], ND[:, j, 1], R[:, j], ALU.mult).then_inc(s["y_ready"], 1)

            def residual(b, j):
                dve.wait_ge(s["yt_ready"], b + 1)
                if b >= 2:
                    dve.wait_ge(s["base_ready"], b - 1)
                dve.tensor_tensor(x1[:, j, :], YT[j], x_all[:, b, :], ALU.add).then_inc(s["x1_ready"], 1)

            def stats(b, j):
                dve.wait_ge(s["x1_ready"], b + 1)
                dve.bn_stats(st2[:, j, :], x1[:, j, :]).then_inc(s["st2_done"], 1)

            def mean_var(b, j):
                dve.wait_ge(s["st2_done"], b + 1)
                if b >= 2:
                    dve.wait_ge(s["nm2_done"], b - 1)
                    dve.wait_ge(s["ve2_done"], b - 1)
                dve.bn_aggr(mv2[:, j, :], st2[:, j, :]).then_inc(s["mv2_done"], 1)

            def variances(b, j):
                dve.wait_ge(s["mv2_done"], b + 1)
                if b >= 2:
                    dve.wait_ge(s["rs2_done"], b - 1)
                dve.scalar_tensor_tensor(out=ve2[:, j, :], in0=var_mul[:, :], scalar=mv2[:, j, 1:2], in1=var_add[:, :],
                                         op0=ALU.mult, op1=ALU.add).then_inc(s["ve2_done"], 1)

            def top_logits(b, j):
                dve.wait_ge(s["lg_ready"], b + 1)
                if b >= 2:
                    dve.wait_ge(s["nmax_done"], b - 1)
                    dve.wait_ge(s["ew_ready"], b - 1)
                dve.max(top8[:, j, :], LG).then_inc(s["top_ready"], 1)

            def top_experts(b, j):
                dve.wait_ge(s["top_ready"], b + 1)
                dve.max_index(idx8[:, j, :], top8[:, j, :], LG).then_inc(s["idx_done"], 1)

            def expert_tags(b, j):
                dve.wait_ge(s["idx_done"], b + 1)
                dve.tensor_scalar(tags[:, b, 0:K], idx8[:, j, 0:K], 1.0, None, ALU.add).then_inc(s["expert_ready"], 1)

            def one_hot(b, j):
                dve.wait_ge(s["expert_ready"], b + 1)
                dve.tensor_tensor(onehot[:, j, :, :], iota_e[:, :].unsqueeze(1).to_broadcast([P, K, E]),
                                  tags[:, b, 0:K].unsqueeze(2).to_broadcast([P, K, E]), ALU.is_equal)\
                    .then_inc(s["onehot_done"], 1)

            def picks_mask(b, j):
                dve.wait_ge(s["onehot_done"], b + 1)
                with nc.allow_low_precision("zeros and ones"):
                    dve.tensor_reduce(mask[:, b, :], onehot[:, j, :, :].rearrange("p k e -> p e k"), AX.X, ALU.add)\
                        .then_inc(s["mask_ready"], 1)

            def next_slots(b, j):
                dve.wait_ge(s["pos_ready"], b + 1)
                dve.tensor_tensor(slots[:, j, :], PO, slot0[:, :], ALU.add).then_inc(s["slots_done"], 1)

            def picked_slots(b, j):
                dve.wait_ge(s["slots_done"], b + 1)
                dve.tensor_tensor(picked[:, j], onehot[:, j, :, :], slots[:, j, :].unsqueeze(1).to_broadcast([P, K, E]),
                                  ALU.mult).then_inc(s["picked_done"], 1)

            def slot_numbers(b, j):
                dve.wait_ge(s["picked_done"], b + 1)
                with nc.allow_low_precision("row numbers are whole numbers below 2^15"):
                    dve.tensor_reduce(slot_all[:, b, :], picked[:, j], AX.X, ALU.add).then_inc(s["slot_ready"], 1)

            run([(0, scan), (3, top_logits), (0, num_den), (3, top_experts), (1, newton_product), (3, expert_tags),
                 (1, newton_step), (3, one_hot), (1, quotient), (3, picks_mask), (-1, times_v),
                 (-1, others_stats), (0, others_shift), (1, residual),
                 (3, next_slots), (1, stats), (3, picked_slots), (1, mean_var), (3, slot_numbers), (1, variances)])

            dve.wait_ge(s["sh_s"], 1)
            dve.tensor_tensor(sg_all[:, :, :], sg_all[:, :, :], gu_all[:, 1], ALU.mult).then_inc(s["sh_a"], 1)
            dve.wait_ge(s["tot_ready"], 1)
            dve.tensor_scalar(big[:, :], TOT, CAP / 2 + 0.5, None, ALU.is_gt).then_inc(s["big_done"], 1)
            for c in range(B // 2):
                dve.wait_ge(s["sh_y"], c + 1)
                dve.wait_ge(s["base_ready"], 2 * c + 2)
                dve.tensor_tensor(base_all[:, 2 * c:2 * c + 2, :], base_all[:, 2 * c:2 * c + 2, :], FY[c % 2],
                                  ALU.add).then_inc(s["sh_b"], 1)
            dve.wait_ge(s["ew_ready"], B)
            dve.reciprocal(rsum[:, :], esum[:, :]).then_inc(s["rsum_done"], 1)
            dve.wait_ge(s["rsum_done"], 1)
            dve.tensor_tensor(w_all[:, :, :], ew[:, :, :], rsum[:, :].unsqueeze(2).to_broadcast([P, B, K]), ALU.mult)\
                .then_inc(s["w_done"], 1)

            dve.wait_ge(s["slot_ready"], B)
            dve.wait_ge(s["expert_ready"], B)
            dve.wait_ge(s["pickno_ready"], 1)
            dve.scalar_tensor_tensor(out=beyond[:, :, :], in0=tags[:, :, 0:K], scalar=float(-ROWS_E),
                                     in1=slot_all[:, :, :], op0=ALU.mult, op1=ALU.add).then_inc(s["beyond_done"], 1)
            dve.wait_ge(s["beyond_done"], 1)
            dve.tensor_reduce(slot_max[:, :], beyond[:, :, :].rearrange("p b k -> p (b k)"), AX.X, ALU.max)\
                .then_inc(s["slot_max_done"], 1)
            dve.tensor_scalar(fits[:, :, :], beyond[:, :, :], float(CAP - ROWS_E), float(OUTSIDE), ALU.is_lt, ALU.mult)\
                .then_inc(s["fits_done"], 1)
            dve.wait_ge(s["fits_done"], 1)
            dve.scalar_tensor_tensor(out=last_all[:, :].rearrange("p (b k) -> p b k", b=B), in0=fits[:, :, :], scalar=-1.0,
                                     in1=tags[:, :, 0:K], op0=ALU.add, op1=ALU.add).then_inc(s["last_all_done"], 1)
            dve.scalar_tensor_tensor(out=late_all[:, :].rearrange("p (b k) -> p b k", b=B), in0=fits[:, :, :],
                                     scalar=float(OUTSIDE), in1=tags[:, :, K:2 * K], op0=ALU.add, op1=ALU.add)\
                .then_inc(s["last_all_done"], 1)
            dve.wait_ge(s["slot_top_done"], 1)
            dve.tensor_scalar(overflow[:, :], slot_top[:, :], float(CAP - ROWS_E), None, ALU.is_ge)\
                .then_inc(s["overflow_done"], 1)

            def picks_of_slots(e, q, n):
                dve.wait_ge(xg_in[q], 16 * (n + 1))
                if later(e, WB):
                    dve.wait_ge(row_out[q], 32 * n)
                dve.scalar_tensor_tensor(out=own[:, q], in0=xg[q][:, :, C:C + K], scalar=iota_e[:, bass.ds(e, 1)],
                                         in1=xg[q][:, :, C + K:RW], op0=ALU.is_equal, op1=ALU.mult)\
                    .then_inc(s["own_done"], 1)
                dve.wait_ge(s["own_done"], e + 1)
                dve.tensor_reduce(owned[:, q], own[:, q], AX.X, ALU.add).then_inc(s["owned_done"], 1)
                dve.wait_ge(s["owned_done"], e + 1)
                dve.tensor_scalar(pick_idx[:, q, :], owned[:, q], float(OUTSIDE), None, ALU.add)\
                    .then_inc(s["pick_ready"], 1)

            def gated(e, j):
                dve.wait_ge(s["f_s"], e + 1)
                if later(e, 2):
                    dve.wait_ge(s["f_y"], e - 1)
                dve.tensor_tensor(act_t[:, j, :], sg[:, j, :], FG[j][:, 1, :], ALU.mult).then_inc(s["f_a"], 1)

            def rows_out_to_sbuf(e, q, n):
                dve.wait_ge(s["f_y"], e + 1)
                if later(e, WB):
                    dve.wait_ge(row_out[q], 32 * n)
                    dve.wait_ge(last_stored[q], 16 * n)
                dve.tensor_copy(yo[:, q, :, :], FY[q % 2]).then_inc(s["f_yo"], 1)

            for e in range(WB):
                picks_of_slots(e, e, 0)
                gated(e, e % 2)
                if e:
                    rows_out_to_sbuf(e - 1, e - 1, 0)
            with dve.Fori(1, E // WB - 1) as i:
                for q in range(WB):
                    picks_of_slots(WB * i + q, q, i)
                    gated(WB * i + q, q % 2)
                    rows_out_to_sbuf(WB * i + q - 1, (q - 1) % WB, i - (q == 0))
            for e in range(E - WB, E):
                picks_of_slots(e, e % WB, e // WB)
                gated(e, e % 2)
                rows_out_to_sbuf(e - 1, (e - 1) % WB, (e - 1) // WB)
            rows_out_to_sbuf(E - 1, WB - 1, E // WB - 1)

            dve.wait_ge(s["sh_b"], B // 2)
            dve.wait_ge(s["w_done"], 1)

            mine = [b for b in range(B) if b not in POOL_SUMS]
            for n, b in enumerate(mine):
                dve.wait_ge(gathered[b], 16)
                for k in range(K):
                    src = base_all[:, b, :] if k == 0 else part[:, n % 2, k - 1, :]
                    dst = res[:, b, :] if k == K - 1 else part[:, n % 2, k, :]
                    if k:
                        dve.wait_ge(s["tail_part"], (K - 1) * n + k)
                    if b == B - 1 and k == K // 2:
                        dve.wait_ge(gathered[B], 16)
                    dve.scalar_tensor_tensor(out=dst, in0=G[:, b, k, :], scalar=w_all[:, b, k:k + 1], in1=src,
                                             op0=ALU.mult, op1=ALU.add)\
                        .then_inc(s["res_ready" if k == K - 1 else "tail_part"], 1)

        @block.tensor
        def _(pe):
            pe.wait_ge(s["ident_set"], 2)
            pe.wait_ge(s["col_in"], 48)
            nc.tensor.transpose(COLT, rows6[:, :], ident[0:3 * HC, 0:3 * HC]).then_inc(s["colT_ready"], 1)
            pe.wait_ge(s["gw_in"], 16)
            pe.wait_ge(s["cols6_done"], 1)
            for h in range(HC):
                last = nc.tensor.transpose(GWT[:, h, :], gw[:, h * P:(h + 1) * P], ident[0:E, 0:E])
            last.then_inc(s["gwT_ready"], 1)
            pe.wait_ge(s["gwT_done"], 1)
            pe.wait_ge(s["tri_set"], 2)
            pe.wait_ge(s["consts"], 9)

            def to_channels(b, j):
                pe.wait_ge(s["ekv_ready"], b + 1)
                if b >= 2:
                    pe.wait_ge(s["nd_done"], 2 * b - 2)
                    pe.wait_ge(s["col0_done"], b - 1)
                for a, src in enumerate((ek, ekv)):
                    for h in range(HC):
                        last = nc.tensor.transpose(XT[j][:, a, h, :], src[:, j, h * P:(h + 1) * P], ident[:, :])
                last.then_inc(s["xt_ready"], 1)

            def to_tokens(b, j):
                pe.wait_ge(s["y_ready"], b + 1)
                if b >= 2:
                    pe.wait_ge(s["x1_ready"], b - 1)
                for h in range(HC):
                    last = nc.tensor.transpose(YT[j][:, h * P:(h + 1) * P], Y[:, j, h, :], ident[:, :])
                last.then_inc(s["yt_ready"], 1)

            def normed_to_channels(b, j):
                pe.wait_ge(s["n_ready"], b + 1)
                if b >= 2:
                    pe.wait_ge(s["hT_ready"], HC * (b - 1))
                for h in range(HC):
                    last = nc.tensor.transpose(NT[j][:, h, :], n_row[:, b, h * P:(h + 1) * P], ident[:, :])
                last.then_inc(s["nt_ready"], 1)

            def logits(b, j):
                pe.wait_ge(s["hT_ready"], HC * (b + 1))
                if b >= 1:
                    pe.wait_ge(s["idx_done"], b)
                    pe.wait_ge(s["slots_done"], b)
                for h in range(HC):
                    last = nc.tensor.matmul(LG, hT[:, j, h, :], gwT[:, h, :], start=(h == 0), stop=(h == HC - 1))
                last.then_inc(s["lg_ready"], 1)

            def positions(b, j):
                pe.wait_ge(s["mask_ready"], b + 1)
                if b >= 1:
                    pe.wait_ge(s["slots_done"], b)
                last = nc.tensor.matmul(PO, tri[:, :], mask[:, b, :], start=True, stop=(b == 0))
                for earlier in range(b):
                    last = nc.tensor.matmul(PO, ones[:, :], mask[:, earlier, :], start=False, stop=(earlier == b - 1))
                last.then_inc(s["pos_ready"], 1)

            def shared_up(b, j):
                if b == 0:
                    pe.wait_ge(s["sh_in"], 32)
                else:
                    pe.wait_ge(s["gu_done"], b)
                for a in range(2):
                    for h in range(HC):
                        last = nc.tensor.matmul(SGU[:, a, :], sgu[:, h, a, :], hT[:, j, h, :],
                                                start=(h == 0), stop=(h == HC - 1))
                last.then_inc(s["gu_ready"], 1)

            run([(3, shared_up), (2, normed_to_channels), (1, to_tokens), (3, positions), (-1, to_channels), (2, logits)])

            pe.wait_ge(s["slots_done"], B)
            for b in range(B):
                last = nc.tensor.matmul(TOT, ones[:, :], mask[:, b, :], start=(b == 0), stop=(b == B - 1))
            last.then_inc(s["tot_ready"], 1)
            pe.wait_ge(s["sh_a"], 1)
            pe.wait_ge(scattered[SHARED_AFTER], 16 * K)
            pe.wait_ge(s["sdn_in"], 16)
            for c in range(B // 2):
                if c >= 2:
                    pe.wait_ge(s["sh_b"], c - 1)
                for a in range(2):
                    last = nc.tensor.matmul(FY[c % 2][:, a, :], sg_all[:, 2 * c + a, :], sdn[:, :], start=True, stop=True)
                last.then_inc(s["sh_y"], 1)
            for j in range(2):
                for a in range(2):
                    nc.tensor.matmul(FG[j][:, a, :], sg_all[:, a, :], sdn[:, :], start=True, stop=True)
            pe.wait_ge(s["nd_done"], 2 * B)
            pe.wait_ge(s["big_done"], 1)

            def rows_to_channels(e, q, n):
                pe.wait_ge(xg_in[q], 16 * (n + 1))
                if e >= 2:
                    pe.wait_ge(s["f_x"], 2 * e - 2)
                for h in range(HC):
                    for a in range(2):
                        last = nc.tensor.transpose(FX[q % 2][:, h, a * P:(a + 1) * P], xg[q][:, a, h * P:(h + 1) * P],
                                                   ident[:, :])
                last.then_inc(s["f_xt"], 1)

            def gate_up_half(q, a, cols):
                for h in range(HC):
                    last = nc.tensor.matmul(FG[q % 2][:, a, cols], w13b[q][:, h, a, :], xT[:, q % 2, h, cols],
                                            start=(h == 0), stop=(h == HC - 1))
                return last

            def gate_up(e, q, n, second):
                pe.wait_ge(w_in[q], 16 * (n + 1))
                pe.wait_ge(s["f_x"], 2 * e + 2)
                if e >= 2:
                    pe.wait_ge(s["f_a"], e - 1)
                with pe.If(second != 0):
                    for a in range(2):
                        gate_up_half(q, a, slice(P, 2 * P))
                for a in range(2):
                    last = gate_up_half(q, a, slice(0, P))
                last.then_inc(s["f_g"], 1)

            def down_half(e, q, a):
                return nc.tensor.matmul(FY[q % 2][:, a, :], act_t[:, q % 2, a * P:(a + 1) * P],
                                        w2_all[:, bass.ds(e, 1), :].rearrange("p o c -> p (o c)"), start=True, stop=True)

            def down(e, q, second):
                pe.wait_ge(s["f_a"], e + 1)
                if e >= 2:
                    pe.wait_ge(s["f_yo"], e - 1)
                with pe.If(second != 0):
                    down_half(e, q, 1)
                down_half(e, q, 0).then_inc(s["f_y"], 1)

            for g in range(W2L):
                pe.wait_ge(w2_in[g], 16)
            second = {}
            rows_to_channels(0, 0, 0)
            for e in range(E + 1):
                if e + 1 < E:
                    rows_to_channels(e + 1, (e + 1) % WB, (e + 1) // WB)
                if e < E:
                    second[e] = pe.value_load(big[0:1, e:e + 1], min_val=0, max_val=1)
                    gate_up(e, e % WB, e // WB, second[e])
                if e:
                    down(e - 1, (e - 1) % WB, second.pop(e - 1))


_INS = ['x', 'ctx_2048', 'L0_xattn_time_decay', 'L0_xattn_time_first', 'L0_ffn_norm_w', 'L0_ffn_gate_w',
        'L0_ffn_w13', 'L0_ffn_w2', 'L0_ffn_shared_gate_w', 'L0_ffn_shared_up_w', 'L0_ffn_shared_down_w']


def kernel(**inputs):
    import numpy as _np
    import concourse.bacc as _bacc
    from concourse import mybir as _mybir
    from concourse.bass_utils import run_bass_kernel_spmd as _run

    nc = _bacc.Bacc("TRN2", target_bir_lowering=False, num_devices=1)
    arrays, args = {}, []
    for name in _INS:
        a = _np.ascontiguousarray(inputs[name])
        arrays[f"in_{name}_dram"] = a
        args.append(nc.dram_tensor(f"in_{name}_dram", a.shape, _mybir.dt.from_np(a.dtype), kind="ExternalInput").ap())
    args.append(nc.dram_tensor("out_dram", (B, T, C), _mybir.dt.float32, kind="ExternalOutput").ap())
    xattn_moe(nc, *args)
    r = _run(nc, [arrays], core_ids=[0])
    return r.results[0]["out_dram"]
```
